# Optimizing a Trainium2 kernel written in Bass

```python
import numpy as np
import jax
import jax.numpy as jnp

def _softmax(x, axis=-1):
    return jax.nn.softmax(x, axis=axis)

def _gelu(x):
    return jax.nn.gelu(x, approximate=True)

def _silu(x):
    return jax.nn.silu(x)

def _sigmoid(x):
    return jax.nn.sigmoid(x)

def _layernorm(x, axis=-1, eps=1e-05):
    m = jnp.mean(x, axis=axis, keepdims=True)
    v = jnp.var(x, axis=axis, keepdims=True)
    return (x - m) / jnp.sqrt(v + eps)

def _scatter_add(tgt, idx, src, axis=0):
    return tgt.at[idx].add(src)

def _segment_sum(src, seg, n):
    return jax.ops.segment_sum(src, seg, n)
kernel_name = 'mk_adaln_d1_jaxref_r8_eabaec'

def setup_inputs(seed: int=0):
    np.random.seed(seed)
    _w = jnp.asarray

    def _L0_attn_setup():
        import jax, jax.numpy as jnp
        import numpy as np
        D_MODEL = 128
        N_HEADS = 16
        K_TOP = 64
        D_HEAD = D_MODEL // N_HEADS
        key = jax.random.key(seed)
        ks = jax.random.split(key, 9)
        B, L = (8, 512)
        bound = 1.0 / np.sqrt(D_MODEL)
        lin = lambda k: jax.random.uniform(k, (D_MODEL, D_MODEL), jnp.float32, -bound, bound)
        vec = lambda k: jax.random.uniform(k, (D_MODEL,), jnp.float32, -bound, bound)
        return {'query': jax.random.normal(ks[0], (B, L, D_MODEL), jnp.float32), 'Wq': lin(ks[1]), 'bq': vec(ks[2]), 'Wk': lin(ks[3]), 'bk': vec(ks[4]), 'Wv': lin(ks[5]), 'bv': vec(ks[6]), 'Wo': lin(ks[7]), 'bo': vec(ks[8])}
    _L0_attn_in = _L0_attn_setup()

    def _L0_ffn_setup():
        import jax, jax.numpy as jnp
        import numpy as np
        B, L, D = (1, 256, 128)
        E, H, G, K = (64, 32, 64, 16)

        def _grouped_routing_scores(router_scores):
            T, En = router_scores.shape
            Tq = T // G
            budget = Tq * K
            order = jnp.argsort(-router_scores, axis=0)
            sorted_vals = jnp.take_along_axis(router_scores, order, axis=0)
            group_score = sorted_vals.reshape(Tq, G, En).sum(axis=1)
            _, top_flat = jax.lax.top_k(group_score.reshape(-1), budget)
            gmask = jnp.zeros((Tq * En,), bool).at[top_flat].set(True).reshape(Tq, En)
            mask_sorted = jnp.broadcast_to(gmask[:, None, :], (Tq, G, En)).reshape(T, En)
            mask = jnp.zeros((T, En), bool).at[order, jnp.arange(En)[None, :]].set(mask_sorted)
            fs = jnp.where(mask, router_scores, 0.0)
            return fs / (fs.sum(axis=-1, keepdims=True) + 1e-06)
        key = jax.random.key(seed)
        ks = jax.random.split(key, 6)
        s = lambda k, shape, scale: jax.random.normal(k, shape, jnp.float32) * scale
        return {'x': jax.random.normal(ks[0], (B, L, D), jnp.float32), 'Wr': s(ks[1], (D, E), D ** (-0.5)), 'br': jnp.zeros((E,), jnp.float32), 'Wup': s(ks[2], (E, D, H), D ** (-0.5)), 'bup': jnp.zeros((E, H), jnp.float32), 'Wgate': s(ks[3], (E, D, H), D ** (-0.5)), 'bgate': jnp.zeros((E, H), jnp.float32), 'Wdown': s(ks[4], (E, H, D), H ** (-0.5)), 'bdown': jnp.zeros((E, D), jnp.float32)}
    _L0_ffn_in = _L0_ffn_setup()
    _L0_c = _w((lambda *s: np.random.randn(*s).astype(np.float32) * 0.05)(4, 128))
    _L0_wmod = _w((lambda *s: np.random.randn(*s).astype(np.float32) * 0.05)(128, 6 * 128) * 128 ** (-0.5))
    _d = {'L0_attn_query': _L0_attn_in['query'], 'L0_attn_Wq': _L0_attn_in['Wq'], 'L0_attn_bq': _L0_attn_in['bq'], 'L0_attn_Wk': _L0_attn_in['Wk'], 'L0_attn_bk': _L0_attn_in['bk'], 'L0_attn_Wv': _L0_attn_in['Wv'], 'L0_attn_bv': _L0_attn_in['bv'], 'L0_attn_Wo': _L0_attn_in['Wo'], 'L0_attn_bo': _L0_attn_in['bo'], 'L0_ffn_Wr': _L0_ffn_in['Wr'], 'L0_ffn_br': _L0_ffn_in['br'], 'L0_ffn_Wup': _L0_ffn_in['Wup'], 'L0_ffn_bup': _L0_ffn_in['bup'], 'L0_ffn_Wgate': _L0_ffn_in['Wgate'], 'L0_ffn_bgate': _L0_ffn_in['bgate'], 'L0_ffn_Wdown': _L0_ffn_in['Wdown'], 'L0_ffn_bdown': _L0_ffn_in['bdown'], 'L0_c': _L0_c, 'L0_wmod': _L0_wmod}
    _x0 = _d['L0_attn_query']
    _d['L0_attn_query'] = jax.random.normal(jax.random.fold_in(jax.random.key(seed), 1), (4, 1024, 128), dtype=_x0.dtype)
    del _x0
    return _d

def reference(L0_attn_query, L0_attn_Wq, L0_attn_bq, L0_attn_Wk, L0_attn_bk, L0_attn_Wv, L0_attn_bv, L0_attn_Wo, L0_attn_bo, L0_ffn_Wr, L0_ffn_br, L0_ffn_Wup, L0_ffn_bup, L0_ffn_Wgate, L0_ffn_bgate, L0_ffn_Wdown, L0_ffn_bdown, L0_c, L0_wmod):

    def _L0_attn_ref(query, Wq, bq, Wk, bk, Wv, bv, Wo, bo):
        import jax, jax.numpy as jnp
        import numpy as np
        D_MODEL = 128
        N_HEADS = 16
        K_TOP = 64
        D_HEAD = D_MODEL // N_HEADS
        B, L_q, D = query.shape
        L_k = L_q
        F_q = L_q // 2 + 1
        F_k = L_k // 2 + 1
        k_top = min(K_TOP, F_q)

        def proj(x, W, b):
            return (x @ W + b).reshape(B, -1, N_HEADS, D_HEAD).transpose(0, 2, 1, 3)
        q = proj(query, Wq, bq)
        k = proj(query, Wk, bk)
        v = proj(query, Wv, bv)
        q_freq = jnp.fft.rfft(q, axis=2)
        k_freq = jnp.fft.rfft(k, axis=2)
        v_freq = jnp.fft.rfft(v, axis=2)
        q_energy = jnp.abs(q_freq).mean(axis=-1)
        _, idx = jax.lax.top_k(q_energy, k_top)
        mapped_idx = jnp.clip(jnp.round(idx.astype(jnp.float32) * (F_k - 1) / (F_q - 1)).astype(jnp.int32), 0, F_k - 1)
        gather = lambda x, i: jnp.take_along_axis(x, i[..., None], axis=2)
        q_top = gather(q_freq, idx)
        k_top_freq = gather(k_freq, mapped_idx)
        v_top = gather(v_freq, mapped_idx)
        eps = 1e-08
        attn_score = (q_top.real * k_top_freq.real).sum(-1) / (D_HEAD ** 0.5 + eps)
        attn = jax.nn.softmax(attn_score, axis=-1)[..., None]
        q_mean_freq = q_freq.mean(axis=2, keepdims=True)
        out_freq = jnp.broadcast_to(q_mean_freq, (B, N_HEADS, F_q, D_HEAD))
        src = (attn * v_top.real).astype(out_freq.dtype)
        bi = jnp.arange(B)[:, None, None]
        hi = jnp.arange(N_HEADS)[None, :, None]
        out_freq = out_freq.at[bi, hi, idx].set(src)
        out_time = jnp.fft.irfft(out_freq, n=L_q, axis=2)
        out = out_time.transpose(0, 2, 1, 3).reshape(B, L_q, D)
        return out @ Wo + bo

    def _L0_ffn_ref(x, Wr, br, Wup, bup, Wgate, bgate, Wdown, bdown):
        import jax, jax.numpy as jnp
        import numpy as np
        B, L, D = (1, 256, 128)
        E, H, G, K = (64, 32, 64, 16)

        def _grouped_routing_scores(router_scores):
            T, En = router_scores.shape
            Tq = T // G
            budget = Tq * K
            order = jnp.argsort(-router_scores, axis=0)
            sorted_vals = jnp.take_along_axis(router_scores, order, axis=0)
            group_score = sorted_vals.reshape(Tq, G, En).sum(axis=1)
            _, top_flat = jax.lax.top_k(group_score.reshape(-1), budget)
            gmask = jnp.zeros((Tq * En,), bool).at[top_flat].set(True).reshape(Tq, En)
            mask_sorted = jnp.broadcast_to(gmask[:, None, :], (Tq, G, En)).reshape(T, En)
            mask = jnp.zeros((T, En), bool).at[order, jnp.arange(En)[None, :]].set(mask_sorted)
            fs = jnp.where(mask, router_scores, 0.0)
            return fs / (fs.sum(axis=-1, keepdims=True) + 1e-06)
        Bx, Lx, Dx = x.shape
        xt = x.reshape(-1, Dx)
        router_scores = jax.nn.softmax(xt @ Wr + br, axis=-1)
        fs = _grouped_routing_scores(router_scores)
        up = jnp.einsum('td,edh->teh', xt, Wup) + bup
        gate = jnp.einsum('td,edh->teh', xt, Wgate) + bgate
        h = jax.nn.silu(up) * gate * fs[:, :, None]
        out = jnp.einsum('teh,ehd->td', h, Wdown) + fs @ bdown
        return out.reshape(Bx, Lx, Dx)
    x = L0_attn_query
    mod = (_silu(L0_c) @ L0_wmod).reshape(L0_c.shape[0], 6, 1, -1)
    sa, ca, ga, sb, cb, gb = (mod[:, 0], mod[:, 1], mod[:, 2], mod[:, 3], mod[:, 4], mod[:, 5])
    ga = (2 * (ga >= 0) - 1) * jnp.maximum(jnp.abs(ga), 0.25)
    gb = (2 * (gb >= 0) - 1) * jnp.maximum(jnp.abs(gb), 0.25)
    h = _layernorm(x, axis=-1) * (1 + ca) + sa
    x = x + ga * _L0_attn_ref(h, L0_attn_Wq, L0_attn_bq, L0_attn_Wk, L0_attn_bk, L0_attn_Wv, L0_attn_bv, L0_attn_Wo, L0_attn_bo)
    h = _layernorm(x, axis=-1) * (1 + cb) + sb
    x = x + gb * _L0_ffn_ref(h, L0_ffn_Wr, L0_ffn_br, L0_ffn_Wup, L0_ffn_bup, L0_ffn_Wgate, L0_ffn_bgate, L0_ffn_Wdown, L0_ffn_bdown)
    return x

_drawn_inputs = setup_inputs


def setup_inputs(seed=0):
    import zlib

    import numpy as np

    out = dict(_drawn_inputs(seed))
    spreads = {'L0_ffn_br': (0.0, 0.8),
     'L0_ffn_bup': (0.0, 0.8),
     'L0_ffn_bgate': (0.0, 0.8),
     'L0_ffn_bdown': (0.0, 0.8)}
    factors = {'L0_attn_Wq': 8.0,
     'L0_attn_bq': 8.0,
     'L0_attn_Wk': 8.0,
     'L0_attn_bk': 8.0,
     'L0_attn_Wv': 8.0,
     'L0_attn_bv': 8.0,
     'L0_attn_Wo': 8.0,
     'L0_attn_bo': 4.181}
    for name, (base, spread) in spreads.items():
        noise = np.random.default_rng([zlib.crc32(name.encode()), seed]).standard_normal(out[name].shape)
        drawn = base * np.exp(spread * noise) if base else spread * noise
        out[name] = jnp.asarray(drawn.astype(out[name].dtype))
    for name, factor in factors.items():
        out[name] = (out[name] * factor).astype(out[name].dtype)
    return out
```

```python
from contextlib import ExitStack

import numpy as np

import concourse.bass as bass
from concourse import mybir

ALU = mybir.AluOpType
ACT = mybir.ActivationFunctionType
F32 = mybir.dt.float32
I32 = mybir.dt.int32
AX = mybir.AxisListType

P = 128
B, L, D = 4, 1024, 128
HEADS, DH = 16, 8
KTOP = 64
A = L // P
AH = A // 2
HALF = L // 2
NF = L // 2 + 1
NRE = (HALF // 2 + 1, HALF // 2)
BH = B * HEADS
E, H, G, KSEL = 64, 32, 64, 16
TOK = B * L
TILES = TOK // P
KT = E * H // P
CH = 512
NCH = TOK // CH
TPC = CH // P
HT = TOK // 2
NG = HT // G
GROUPS = TOK // G * KSEL
EPS = 1e-5
RATIO = 16
SHIFTS = (27, 23, 19, 15, 11, 7, 3, 0)
NEVER = 1e30

C_ID, C_ONE, C_SGN, C_SEL, C_EXP = 0, P, 2 * P, 2 * P + 1, 2 * P + 1 + B * BH
C_ALL = C_EXP + B * P
V_C, V_UP, V_GATE, V_ALL = 0, B, B + KT, B + 2 * KT
W_Q, W_K, W_V, W_O, W_L, W_ALL = 0, P, 2 * P, 3 * P, 4 * P, 4 * P + 1


def transform_tables():
    t = np.arange(HALF)[:, None]
    fwd, inv = [], []
    for par in range(2):
        fre = 2 * np.arange(NRE[par])[None, :] + par
        fim = fre[:, 1:HALF // 2] if par == 0 else fre
        are, aim = 2 * np.pi * ((t * fre) % L) / L, 2 * np.pi * ((t * fim) % L) / L
        fwd.append(np.concatenate([np.cos(are), -np.sin(aim)], axis=1))
        weight = np.where((fre == 0) | (fre == HALF), 1.0, 2.0)
        inv.append(np.concatenate([weight * np.cos(are), -2.0 * np.sin(aim)], axis=1).T / L)
    fwd = np.stack(fwd, axis=1).reshape(AH, P, 2, HALF).transpose(1, 0, 2, 3)
    inv = np.concatenate(inv, axis=0).reshape(A, P, HALF).transpose(1, 0, 2)
    return (np.ascontiguousarray(fwd.reshape(P, -1), dtype=np.float32),
            np.ascontiguousarray(inv.reshape(P, -1), dtype=np.float32))


def constants():
    c = np.zeros((P, C_ALL), np.float32)
    c[:, C_ID:C_ID + P] = np.eye(P)
    c[:, C_ONE:C_ONE + P] = 1.0
    c[:, C_SGN] = np.where(np.arange(P) < E, 1.0, -1.0)
    for b in range(B):
        for ch in range(D):
            row = b * HEADS + ch // DH
            c[ch, C_SEL + b * BH + row] = 1.0
            c[row, C_EXP + b * P + ch] = 1.0
    return c


def round_bits():
    bits = np.zeros((len(SHIFTS), RATIO), np.int32)
    for r, s in enumerate(SHIFTS):
        width = (SHIFTS[r - 1] if r else 31) - s
        bits[r] = np.minimum(np.arange(RATIO), 2 ** width - 1).astype(np.int32) << s
    return np.ascontiguousarray(np.broadcast_to(bits.reshape(1, -1), (P, bits.size)))


def build(nc, x, cst, bits, cols, rows, wmod, wqkv, wo, tabf, tabi, wr, br, wup, wgate, wdown, bdown, out):
    with ExitStack() as ctx:
        def sb(name, shape, dt=F32):
            return ctx.enter_context(nc.sbuf_tensor(name, shape, dt))

        def sem(name):
            return ctx.enter_context(nc.semaphore(name))

        bank = [ctx.enter_context(nc.psum_tensor(f"bank{i}", [P, 512], F32)) for i in range(8)]

        x_sb = sb("x_sb", [P, B, A, D])
        xn = sb("xn", [P, A, B, D])
        region_fold = sb("region_fold", [P, 2, AH, B * D])
        fold = region_fold
        h2t = region_fold[:, :, :, :].rearrange("p s a n -> p (s a n)")
        region_table = sb("region_table", [P, 2, HT])
        tabf_sb = region_table[:, :, :].rearrange("p s (a c) -> p (s a c)", a=2).rearrange(
            "p (a s c) -> p a s c", a=AH, s=2)
        keys = region_table
        tabi_sb = sb("tabi_sb", [P, A, HALF])
        region_freq = sb("region_freq", [P, B, 2, HALF])
        xf = region_freq
        flat_freq = region_freq[:, :, :, :].rearrange("p b s n -> p (b s n)")
        prob = flat_freq[:, 0:HT].rearrange("p (j h e) -> p j h e", h=2, e=E)
        probt = flat_freq[:, HT:2 * HT]
        region_q = sb("region_q", [P, B, 2, HALF])
        qf = region_q
        gated = region_q[:, :, :, :].rearrange("p b s n -> p (b s n)")
        of = sb("of", [P, B, 2, HALF])
        vf = sb("vf", [P, B, NF])
        yf = sb("yf", [P, A, B * D])

        cst_sb = sb("cst_sb", [P, C_ALL])
        bits_sb = sb("bits_sb", [P, len(SHIFTS) * RATIO], I32)
        cols_sb = sb("cols_sb", [P, V_ALL])
        rows_sb = sb("rows_sb", [1, W_ALL])
        wmod_sb = sb("wmod_sb", [P, 6 * D])
        wqkv_sb = sb("wqkv_sb", [P, 3, D])
        wo_sb = sb("wo_sb", [P, D])
        wr_sb = sb("wr_sb", [P, E])
        br_sb = sb("br_sb", [P, E])
        wup_sb = sb("wup_sb", [P, KT, P])
        wgate_sb = sb("wgate_sb", [P, KT, P])
        wdown_sb = sb("wdown_sb", [P, KT, D])
        bdown_sb = sb("bdown_sb", [E, D])

        sc = sb("sc", [P, B])
        scb = sb("scb", [P, B, P])
        mods = sb("mods", [P, 6, B])
        camod = sb("camod", [P, 2, B])
        sal = sb("sal", [P, B])
        gsign = sb("gsign", [P, B * D])
        gabs = sb("gabs", [P, B * D])
        gval = sb("gval", [P, B * D])
        gb8 = sb("gb8", [P, B, 2])
        wob = sb("wob", [P, B, D])
        bol = sb("bol", [1, B * D])
        stats = sb("stats", [P, B, A, 6])
        lns = sb("lns", [P, 7, B, 2])
        acc = sb("acc", [P, 2, B, 2])
        qmean = sb("qmean", [P, 2, B])
        top8 = sb("top8", [BH, 8])
        hstat = sb("hstat", [BH, 4])
        sm = sb("sm", [P, 3, 8])
        gsum = sb("gsum", [P, NG])
        gmin = sb("gmin", [P, NG])
        cand = sb("cand", [P, RATIO])
        cnt = sb("cnt", [P, RATIO])
        hit = sb("hit", [P, RATIO])
        tau = sb("tau", [P, 1])
        gpen = sb("gpen", [P, NG])
        vth = sb("vth", [P, 3])
        rden = sb("rden", [P, TILES])

        def carve(region, shape):
            free = list(shape[1:])
            at, size = region[1], int(np.prod(free))
            region[1] += size
            assert region[1] <= region[0].shape[1]
            view = region[0][0:shape[0], at:at + size]
            if len(free) == 2:
                return view.rearrange("p (a b) -> p a b", b=free[1])
            if len(free) == 3:
                return view.rearrange("p (a b c) -> p a b c", b=free[1], c=free[2])
            return view

        before_y = [yf[:, :, :].rearrange("p a n -> p (a n)"), 0]
        sq = carve(before_y, [P, 2, HALF])
        e2 = carve(before_y, [P, 2, NRE[0]])
        mag = carve(before_y, [P, 2, NRE[0]])
        prodqk = carve(before_y, [P, 2, NRE[0]])
        after_y = [yf[:, :, :].rearrange("p a n -> p (a n)"), 0]
        swapped = carve(after_y, [P, HT])
        cmp = carve(after_y, [P, RATIO, NG])
        after_fold = [h2t, 0]
        energy = carve(after_fold, [BH, NF])
        nsel = carve(after_fold, [BH, NF])
        masked = carve(after_fold, [BH, NF])
        attn = carve(after_fold, [BH, NF])
        av = carve(after_fold, [P, NRE[0]])
        after_q = [region_q[:, :, :, :].rearrange("p b s n -> p (b s n)"), 0]
        tsum = carve(after_q, [P, 2, B * D])
        after_of = [of[:, :, :, :].rearrange("p b s n -> p (b s n)"), 0]
        logit = carve(after_of, [P, 2, 8, E])
        silu = carve(after_of, [P, 2, CH])
        glin = carve(after_of, [P, 2, CH])
        after_tabi = [tabi_sb[:, :, :].rearrange("p a n -> p (a n)"), 0]
        hid = carve(after_tabi, [P, 4, CH])
        outt = carve(after_tabi, [P, CH])
        res = carve(after_tabi, [P, TPC, D])

        ident = cst_sb[:, C_ID:C_ID + P]
        ones = cst_sb[:, C_ONE:C_ONE + P]

        ld_c = sem("ld_c")
        ld_x = [sem(f"ld_x{a}") for a in range(AH)]
        ld_mod = sem("ld_mod")
        ld_tabf = sem("ld_tabf")
        ld_w = sem("ld_w")
        ld_tabi = sem("ld_tabi")
        ld_ffn = sem("ld_ffn")
        sc_done = sem("sc_done")
        scb_done = sem("scb_done")
        mod_mm = sem("mod_mm")
        mod_read = sem("mod_read")
        var_ready = sem("var_ready")
        std_ready = sem("std_ready")
        xn_ready = sem("xn_ready")
        plus_ready = sem("plus_ready")
        minus_ready = sem("minus_ready")
        fwd_ready = sem("fwd_ready")
        xf_act = sem("xf_act")
        xf_dve = sem("xf_dve")
        xf_fixed = sem("xf_fixed")
        q_mm = sem("q_mm")
        k_mm = sem("k_mm")
        v_mm = sem("v_mm")
        q_kept = sem("q_kept")
        sq_ready = sem("sq_ready")
        e2_ready = sem("e2_ready")
        mag_ready = sem("mag_ready")
        prod_ready = sem("prod_ready")
        v_kept = sem("v_kept")
        head_sums = sem("head_sums")
        en_read = sem("en_read")
        smax_ready = sem("smax_ready")
        exp_ready = sem("exp_ready")
        attn_ready = sem("attn_ready")
        nsel_ready = sem("nsel_ready")
        qmean_ready = sem("qmean_ready")
        spread = sem("spread")
        oim_ready = sem("oim_ready")
        ore_ready = sem("ore_ready")
        y_mm = sem("y_mm")
        y_act = sem("y_act")
        y_fixed = sem("y_fixed")
        inv_even = sem("inv_even")
        inv_odd = sem("inv_odd")
        inv_read = sem("inv_read")
        tr_mm = sem("tr_mm")
        h2_act = sem("h2_act")
        h2_dve = sem("h2_dve")
        logit_mm = sem("logit_mm")
        logit_read = sem("logit_read")
        centred = sem("centred")
        rexp = sem("rexp")
        prob_ready = sem("prob_ready")
        prob_tr = sem("prob_tr")
        probt_ready = sem("probt_ready")
        cmp_done = sem("cmp_done")
        cnt_mm = sem("cnt_mm")
        gate_half = sem("gate_half")
        gate_dup = sem("gate_dup")
        den_mm = sem("den_mm")
        up_mm = sem("up_mm")
        gate_mm = sem("gate_mm")
        silu_ready = sem("silu_ready")
        gate_used = sem("gate_used")
        hid_ready = sem("hid_ready")
        down_mm = sem("down_mm")
        outt_ready = sem("outt_ready")
        back_mm = sem("back_mm")
        res_ready = sem("res_ready")
        stored = sem("stored")
        dve_chain = sem("dve_chain")

        block = ctx.enter_context(nc.Block())

        def pair(view, a):
            return view[:, :, a:a + AH + 1:AH]

        @block.sync
        def _(sp):
            xv = x.rearrange("b (a p) d -> a p b d", p=P)
            for a in range(AH):
                for t in (a, a + AH):
                    sp.dma_start(x_sb[:, :, t, :], xv[t]).then_inc(ld_x[a], 16)
            sp.dma_start(wqkv_sb[:, :, :], wqkv.rearrange("d (s n) -> d s n", s=3)).then_inc(ld_w, 16)
            sp.dma_start(wo_sb[:, :], wo).then_inc(ld_w, 16)
            sp.dma_start(tabi_sb[:, :, :], tabi.rearrange("p (a n) -> p a n", a=A)).then_inc(ld_tabi, 16)
            sp.dma_start(wr_sb[:, :], wr).then_inc(ld_ffn, 16)
            sp.dma_start(br_sb[:, :], br.partition_broadcast(P)).then_inc(ld_ffn, 16)
            sp.dma_start(bdown_sb[:, :], bdown).then_inc(ld_ffn, 16)
            sp.dma_start(bits_sb[:, :], bits).then_inc(ld_ffn, 16)
            sp.dma_start(wup_sb[:, :, :], wup.rearrange("d (k n) -> d k n", k=KT)).then_inc(ld_ffn, 16)
            sp.dma_start(wgate_sb[:, :, :], wgate.rearrange("d (k n) -> d k n", k=KT)).then_inc(ld_ffn, 16)
            sp.dma_start(wdown_sb[:, :, :], wdown.rearrange("d (k n) -> d k n", k=KT)).then_inc(ld_ffn, 16)
            sp.wait_ge(gate_half, 2)
            sp.dma_start(gated[E:P, 0:HT], gated[0:E, 0:HT]).then_inc(gate_dup, 16)
            sp.dma_start(gated[0:E, HT:TOK], gated[E:P, HT:TOK]).then_inc(gate_dup, 16)
            ov = out.rearrange("b (c j p) d -> (b c) p j d", j=TPC, p=P)
            sp.sem_inc(stored, 16)
            with sp.Fori(0, NCH) as n:
                sp.wait_ge(res_ready, n * TPC + 2 * TPC)
                sp.dma_start(ov[bass.ds(n, 1)].rearrange("o p j d -> (o p) j d"), res[:, :, :]).then_inc(stored, 16)
            sp.wait_ge(stored, 16 * (NCH + 1))

        @block.gpsimd
        def _(pool):
            for a in range(AH):
                pool.wait_ge(xn_ready, a + 1)
                nc.gpsimd.tensor_tensor(fold[:, 1, a, :].rearrange("p (b d) -> p b d", b=B),
                                        xn[:, a], xn[:, a + AH], ALU.subtract).then_inc(minus_ready, 1)

        @block.scalar
        def _(act):
            act.dma_start(cols_sb[:, :], cols).then_inc(ld_c, 16)
            act.dma_start(rows_sb[:, :], rows).then_inc(ld_c, 16)
            act.dma_start(wmod_sb[:, :], wmod).then_inc(ld_mod, 16)
            act.dma_start(cst_sb[:, :], cst).then_inc(ld_c, 16)
            act.dma_start(tabf_sb, tabf.rearrange("p (a s c) -> p a s c", a=AH, s=2)).then_inc(ld_tabf, 16)
            act.wait_ge(ld_c, 48)
            nc.scalar.activation(sc[:, :], cols_sb[:, V_C:V_C + B], ACT.Silu).then_inc(sc_done, 1)

            def std(n):
                act.wait_ge(var_ready, n + 1)
                nc.scalar.activation(lns[:, 5], lns[:, 4], ACT.Sqrt).then_inc(std_ready, 1)

            for a in range(AH):
                std(a)
            for b in range(B):
                act.wait_ge(fwd_ready, 2 * b + 1)
                act.wait_ge(mod_read, 2)
                nc.scalar.activation(xf[:, b, 0, :], bank[2 * b][:, :], ACT.Copy,
                                     scale=camod[:, 0, b:b + 1]).then_inc(xf_act, 1)

            def magnitude(i):
                act.wait_ge(e2_ready, i + 1)
                if i >= 2:
                    act.wait_ge(head_sums, i - 1)
                par = i % 2
                nc.scalar.activation(mag[:, par, 0:NRE[par]], e2[:, par, 0:NRE[par]],
                                     ACT.Sqrt).then_inc(mag_ready, 1)

            for i in range(2 * B):
                b, par = i // 2, i % 2
                n = NRE[par]
                act.wait_ge(q_mm, i + 1)
                nc.scalar.activation(qf[:, b, par, 0:n], bank[par][:, 0:n], ACT.Copy,
                                     accum_out=acc[:, 0, b, par:par + 1])
                nc.scalar.activation(qf[:, b, par, n:HALF], bank[par][:, n:HALF], ACT.Copy,
                                     accum_out=acc[:, 1, b, par:par + 1]).then_inc(q_kept, 1)
                if i >= 2:
                    act.wait_ge(e2_ready, i - 1)
                nc.scalar.activation(sq[:, par, :], bank[par][:, :], ACT.Square).then_inc(sq_ready, 1)
                if i >= 1:
                    magnitude(i - 1)
            magnitude(2 * B - 1)
            act.wait_ge(smax_ready, 1)
            nc.scalar.activation(attn[:, :], masked[:, :], ACT.Exp, bias=hstat[:, 1:2],
                                 scale=1.0 / (DH ** 0.5 + 1e-8), accum_out=hstat[:, 2:3]).then_inc(exp_ready, 1)
            act.wait_ge(qmean_ready, 1)
            for i in range(2 * B):
                par, b = i // B, i % B
                act.wait_ge(spread, i + 1)
                lo = 1 - par
                nc.scalar.activation(of[:, b, par, NRE[par]:HALF], bank[2 + b % 2][:, lo:HALF // 2],
                                     ACT.Copy, scale=qmean[:, 1, b:b + 1]).then_inc(oim_ready, 1)
            for i in range(A):
                act.wait_ge(y_mm, i + 1)
                nc.scalar.copy(yf[:, i, :], bank[4 + i % 4][:, :]).then_inc(y_act, 1)
            for a in range(AH):
                std(AH + a)
            for n in range(0, NCH, 2):
                b = n // 2
                act.wait_ge(tr_mm, n + 1)
                nc.scalar.activation(h2t[:, CH * n:CH * (n + 1)], bank[4 + n % 4][:, :], ACT.Identity,
                                     scale=camod[:, 1, b:b + 1], bias=mods[:, 3, b:b + 1]).then_inc(h2_act, 1)
            for g in range(B):
                act.wait_ge(centred, g + 1)
                nc.scalar.activation(logit[:, g % 2], logit[:, g % 2], ACT.Exp).then_inc(rexp, 1)
            for g in range(4):
                act.wait_ge(prob_tr, g + 1)
                nc.scalar.copy(probt[:, CH * g:CH * (g + 1)], bank[4 + g][:, :]).then_inc(probt_ready, 1)

            def shift_out(n):
                act.wait_ge(down_mm, (n + 1) * KT)
                act.wait_ge(back_mm, n + 1)
                nc.scalar.activation(outt[:, :], bank[4][:, :], ACT.Copy,
                                     scale=gb8[:, :, :].rearrange("p b c -> p (b c)")[:, bass.ds(n, 1)]
                                     ).then_inc(outt_ready, 1)

            def silus(n, first):
                for k in range(KT):
                    if k == 2 and not first:
                        shift_out(n - 1)
                    act.wait_ge(up_mm, n * KT + (k + 1))
                    if not (first and k < 2):
                        act.wait_ge(gate_used, n * KT + (k - 1))
                    nc.scalar.activation(silu[:, k % 2, :], bank[k % 2][:, :], ACT.Silu,
                                         bias=cols_sb[:, V_UP + k:V_UP + k + 1]).then_inc(silu_ready, 1)

            silus(0, True)
            with act.Fori(1, NCH) as n:
                silus(n, False)
            shift_out(NCH - 1)

        @block.vector
        def _(dve):
            steps = [0]

            def link(ins):
                steps[0] += 1
                ins.then_inc(dve_chain, 1)
                dve.wait_ge(dve_chain, steps[0])

            v = nc.vector
            dve.wait_ge(sc_done, 1)
            v.tensor_copy(scb[:, :, :], sc[:, :].unsqueeze(2).broadcast_to([P, B, P])).then_inc(scb_done, 1)

            def ln_stats(a):
                for b in range(B):
                    for t in (a, a + AH):
                        ins = v.bn_stats(stats[:, b, t, :], x_sb[:, b, t, :])
                link(ins)
                st = pair(stats, a)
                me, m2e, mo, m2o = st[:, :, :, 1], st[:, :, :, 2], st[:, :, :, 4], st[:, :, :, 5]
                v.tensor_tensor(lns[:, 0], me, mo, ALU.add)
                v.tensor_tensor(lns[:, 1], me, mo, ALU.subtract)
                link(v.tensor_tensor(lns[:, 2], m2e, m2o, ALU.add))
                v.tensor_scalar(lns[:, 6], lns[:, 0], 0.5, None, ALU.mult)
                v.scalar_tensor_tensor(out=lns[:, 3], in0=lns[:, 1], scalar=0.25, in1=lns[:, 1],
                                       op0=ALU.mult, op1=ALU.mult)
                link(v.tensor_scalar(lns[:, 2], lns[:, 2], 1.0 / D, EPS, ALU.mult, ALU.add))
                v.tensor_tensor(lns[:, 4], lns[:, 3], lns[:, 2], ALU.add).then_inc(var_ready, 1)

            def ln_apply(n, a):
                dve.wait_ge(std_ready, n + 1)
                link(v.reciprocal(lns[:, 5], lns[:, 5]))
                for b in range(B):
                    for s, t in enumerate((a, a + AH)):
                        ins = v.tensor_scalar(xn[:, t, b, :], x_sb[:, b, t, :], lns[:, 6, b, s:s + 1],
                                              lns[:, 5, b, s:s + 1], ALU.subtract, ALU.mult)
                ins.then_inc(xn_ready, 1)

            def modulation():
                dve.wait_ge(mod_mm, 1)
                link(v.tensor_copy(mods[:, :, :], bank[0][:, 0:6 * B].rearrange("p (m b) -> p m b", b=B)))
                v.tensor_scalar(camod[:, 0, :], mods[:, 1, :], 1.0, None, ALU.add)
                v.tensor_scalar(camod[:, 1, :], mods[:, 4, :], 1.0, None, ALU.add)
                v.tensor_scalar(sal[:, :], mods[:, 0, :], float(L), None, ALU.mult)
                link(v.tensor_copy(gval[:, :], bank[1][:, :]))
                dve.sem_inc(mod_read, 1)
                link(away_from_zero(gb8[:, :, 0], mods[:, 5, :], B))
                v.tensor_copy(gb8[:, :, 1], gb8[:, :, 0])
                away_from_zero(gval[:, :], gval[:, :], B * D).then_inc(mod_read, 1)

            def away_from_zero(out_, g, n):
                link(v.tensor_scalar(gsign[:, 0:n], g, 0.0, None, ALU.is_ge))
                v.tensor_scalar(gsign[:, 0:n], gsign[:, 0:n], 2.0, -1.0, ALU.mult, ALU.add)
                link(v.scalar_tensor_tensor(out=gabs[:, 0:n], in0=g, scalar=-1.0, in1=g, op0=ALU.mult, op1=ALU.max))
                return v.scalar_tensor_tensor(out=out_, in0=gabs[:, 0:n], scalar=0.25, in1=gsign[:, 0:n],
                                              op0=ALU.max, op1=ALU.mult)

            for a in range(AH):
                dve.wait_ge(ld_x[a], 32)
                ln_stats(a)
                if a == 0:
                    modulation()
                ln_apply(a, a)
                dve.wait_ge(xn_ready, a + 1)
                v.tensor_tensor(fold[:, 0, a, :].rearrange("p (b d) -> p b d", b=B),
                                xn[:, a], xn[:, a + AH], ALU.add).then_inc(plus_ready, 1)
            dve.wait_ge(ld_w, 32)
            dve.wait_ge(mod_read, 2)
            v.tensor_tensor(wob[:, :, :], wo_sb[:, :].unsqueeze(1).broadcast_to([P, B, D]),
                            gval[:, :].rearrange("p (b d) -> p b d", b=B), ALU.mult)
            link(v.scalar_tensor_tensor(out=bol[:, :].rearrange("p (b d) -> p b d", b=B),
                                        in0=rows_sb[0:1, W_O:W_O + D].unsqueeze(1).broadcast_to([1, B, D]),
                                        scalar=float(L), in1=gval[0:1, :].rearrange("p (b d) -> p b d", b=B),
                                        op0=ALU.mult, op1=ALU.mult))
            for b in range(B):
                dve.wait_ge(fwd_ready, 2 * b + 2)
                v.tensor_scalar(xf[:, b, 1, :], bank[2 * b + 1][:, :], camod[:, 0, b:b + 1], None,
                                ALU.mult).then_inc(xf_dve, 1)
                dve.wait_ge(xf_act, b + 1)
                v.tensor_tensor(xf[:, b, 0, 0:1], xf[:, b, 0, 0:1], sal[:, b:b + 1],
                                ALU.add).then_inc(xf_fixed, 1)
            for i in range(2 * B):
                b, par = i // 2, i % 2
                n = NRE[par]
                if i >= 2:
                    dve.wait_ge(head_sums, i - 1)
                dve.wait_ge(k_mm, i + 1)
                dve.wait_ge(q_kept, i + 1)
                v.tensor_tensor(prodqk[:, par, 0:n], bank[2][:, 0:n], qf[:, b, par, 0:n],
                                ALU.mult).then_inc(prod_ready, 1)
                dve.wait_ge(v_mm, i + 1)
                v.tensor_copy(vf[:, b, par * NRE[0]:par * NRE[0] + n], bank[3][:, 0:n]).then_inc(v_kept, 1)
                dve.wait_ge(sq_ready, i + 1)
                if i >= 2:
                    dve.wait_ge(mag_ready, i - 1)
                if par == 0:
                    v.tensor_copy(e2[:, 0, 0:HALF // 2 + 1:HALF // 2], sq[:, 0, 0:HALF // 2 + 1:HALF // 2])
                    v.tensor_tensor(e2[:, 0, 1:HALF // 2], sq[:, 0, 1:HALF // 2], sq[:, 0, n:HALF],
                                    ALU.add).then_inc(e2_ready, 1)
                else:
                    v.tensor_tensor(e2[:, 1, 0:n], sq[:, 1, 0:n], sq[:, 1, n:HALF],
                                    ALU.add).then_inc(e2_ready, 1)
            v.tensor_tensor(qmean[:, :, :], acc[:, :, :, 0], acc[:, :, :, 1], ALU.add)
            dve.wait_ge(head_sums, 2 * B)
            link(v.tensor_copy(energy[:, 0:NRE[0]], bank[4][0:BH, 0:NRE[0]]))
            link(v.tensor_copy(energy[:, NRE[0]:NF], bank[5][0:BH, 0:NRE[1]]))
            v.tensor_scalar(qmean[:, :, :], qmean[:, :, :], 1.0 / NF, None, ALU.mult).then_inc(qmean_ready, 1)
            for _i in range(KTOP // 8):
                link(v.max(top8[:, :], energy[:, :]))
                link(v.match_replace(energy[:, :], top8[:, :], energy[:, :], -1.0))
            v.tensor_scalar(nsel[:, :], energy[:, :], 0.0, None, ALU.is_ge).then_inc(nsel_ready, 1)
            dve.wait_ge(nsel_ready, 1)
            for s, (lo, hi) in enumerate(((0, NRE[0]), (NRE[0], NF))):
                ins = v.scalar_tensor_tensor(out=masked[:, lo:hi], in0=nsel[:, lo:hi], scalar=-NEVER,
                                             in1=bank[6 + s][0:BH, 0:hi - lo], op0=ALU.mult, op1=ALU.add)
            ins.then_inc(en_read, 1)
            dve.wait_ge(en_read, 1)
            link(v.tensor_reduce(hstat[:, 0:1], masked[:, :], AX.X, ALU.max))
            v.tensor_scalar(hstat[:, 1:2], hstat[:, 0:1], -1.0 / (DH ** 0.5 + 1e-8), None,
                            ALU.mult).then_inc(smax_ready, 1)
            dve.wait_ge(exp_ready, 1)
            link(v.reciprocal(hstat[:, 3:4], hstat[:, 2:3]))
            v.tensor_scalar(attn[:, :], attn[:, :], hstat[:, 3:4], None, ALU.mult).then_inc(attn_ready, 1)
            for i in range(2 * B):
                par, b = i // B, i % B
                n = NRE[par]
                dve.wait_ge(spread, i + 1)
                link(v.tensor_tensor(av[:, 0:n], bank[b % 2][:, 0:n],
                                     vf[:, b, par * NRE[0]:par * NRE[0] + n], ALU.mult))
                dve.wait_ge(oim_ready, i + 1)
                v.scalar_tensor_tensor(out=of[:, b, par, 0:n], in0=bank[2 + b % 2][:, 0:n],
                                       scalar=qmean[:, 0, b:b + 1], in1=av[:, 0:n],
                                       op0=ALU.mult, op1=ALU.add).then_inc(ore_ready, 1)
                dve.wait_ge(ore_ready, i + 1)
            dve.wait_ge(y_act, 1)
            v.tensor_tensor(yf[0:1, 0, :], yf[0:1, 0, :], bol[:, :], ALU.add).then_inc(y_fixed, 1)

            for a in range(AH):
                dve.wait_ge(inv_even, a + 1)
                ev = bank[a % 2][:, :].rearrange("p (b d) -> p b d", b=B)
                od = bank[2 + a % 2][:, :].rearrange("p (b d) -> p b d", b=B)
                ts = [tsum[:, s, :].rearrange("p (b d) -> p b d", b=B) for s in range(2)]
                v.tensor_tensor(ts[0], x_sb[:, :, a, :], ev, ALU.add)
                link(v.tensor_tensor(ts[1], x_sb[:, :, a + AH, :], ev, ALU.add))
                dve.wait_ge(inv_odd, a + 1)
                v.tensor_tensor(x_sb[:, :, a, :], ts[0], od, ALU.add)
                v.tensor_tensor(x_sb[:, :, a + AH, :], ts[1], od, ALU.subtract).then_inc(inv_read, 1)
                dve.wait_ge(inv_read, a + 1)
                ln_stats(a)
                ln_apply(AH + a, a)
            for n in range(1, NCH, 2):
                dve.wait_ge(tr_mm, n + 1)
                v.tensor_scalar(h2t[:, CH * n:CH * (n + 1)], bank[4 + n % 4][:, :], camod[:, 1, n // 2:n // 2 + 1],
                                mods[:, 3, n // 2:n // 2 + 1], ALU.mult, ALU.add).then_inc(h2_dve, 1)

            def bcast(s):
                return s.unsqueeze(2).broadcast_to([P, 8, E])

            def centre(g):
                lg = logit[:, g % 2]
                dve.wait_ge(logit_mm, g + 1)
                v.tensor_tensor(lg, bank[g][:, :].rearrange("p (j e) -> p j e", e=E),
                                br_sb[:, :].unsqueeze(1).broadcast_to([P, 8, E]), ALU.add).then_inc(logit_read, 1)
                dve.wait_ge(logit_read, g + 1)
                link(v.tensor_reduce(sm[:, 0, :], lg, AX.X, ALU.max))
                v.tensor_tensor(lg, lg, bcast(sm[:, 0, :]), ALU.subtract).then_inc(centred, 1)

            def normalise(g):
                lg = logit[:, g % 2]
                dve.wait_ge(rexp, g + 1)
                link(v.tensor_reduce(sm[:, 1, :], lg, AX.X, ALU.add))
                link(v.reciprocal(sm[:, 2, :], sm[:, 1, :]))
                v.tensor_tensor(prob[:, 8 * (g % 2):8 * (g % 2) + 8, g // 2, :], lg, bcast(sm[:, 2, :]),
                                ALU.mult).then_inc(prob_ready, 1)

            centre(0)
            for g in range(1, B):
                centre(g)
                normalise(g - 1)
                dve.wait_ge(prob_ready, g)
            normalise(B - 1)
            for g in range(4):
                dve.wait_ge(probt_ready, g + 1)
                link(v.tensor_scalar(keys[:, 0, CH * g:CH * (g + 1)], probt[:, CH * g:CH * (g + 1)],
                                     cst_sb[:, C_SGN:C_SGN + 1], None, ALU.mult))
            cur = 0

            def exchange(src, dst, dist, mirrored):
                s = keys[:, src, :].rearrange("p (m two d) -> p m two d", two=2, d=dist)
                o = keys[:, dst, :].rearrange("p (m two d) -> p m two d", two=2, d=dist)
                lo, hi = s[:, :, 0, :], s[:, :, 1, :]
                ohi = o[:, :, 1, :]
                if mirrored:
                    hi, ohi = hi[:, :, ::-1], ohi[:, :, ::-1]
                v.tensor_tensor(o[:, :, 0, :], lo, hi, ALU.max)
                link(v.tensor_tensor(ohi, lo, hi, ALU.min))

            dist = 1
            while dist < HT:
                exchange(cur, 1 - cur, dist, True)
                cur = 1 - cur
                d = dist // 2
                while d >= 1:
                    exchange(cur, 1 - cur, d, False)
                    cur = 1 - cur
                    d //= 2
                dist *= 2
            v.tensor_copy(swapped[0:E, :], keys[E:P, cur, :])
            link(v.tensor_copy(swapped[E:P, :], keys[0:E, cur, :]))
            link(v.scalar_tensor_tensor(out=keys[:, 1 - cur, :], in0=swapped[:, :], scalar=-1.0,
                                        in1=keys[:, cur, :], op0=ALU.mult, op1=ALU.max))
            cur = 1 - cur
            d = HT // 2
            while d >= G:
                exchange(cur, 1 - cur, d, False)
                cur = 1 - cur
                d //= 2
            link(v.tensor_scalar(swapped[:, :], keys[:, cur, :], cst_sb[:, C_SGN:C_SGN + 1], None, ALU.mult))
            gv = swapped[:, :].rearrange("p (q g) -> p q g", g=G)
            v.tensor_reduce(gsum[:, :], gv, AX.X, ALU.add)
            v.tensor_reduce(gmin[:, :], gv, AX.X, ALU.min)
            dve.wait_ge(ld_ffn, 112)
            link(v.memset(tau[:, :], 0.0))
            base = steps[0]
            with dve.Fori(0, len(SHIFTS)) as r:
                ti = tau[:, :].bitcast(I32).broadcast_to([P, RATIO])
                v.tensor_tensor(cand[:, :].bitcast(I32), ti, bits_sb[:, bass.ds(r * RATIO, RATIO)],
                                ALU.bitwise_or).then_inc(dve_chain, 1)
                dve.wait_ge(dve_chain, r * 4 + (base + 1))
                v.tensor_tensor(cmp[:, :, :], gsum[:, :].unsqueeze(1).broadcast_to([P, RATIO, NG]),
                                cand[:, :].unsqueeze(2).broadcast_to([P, RATIO, NG]),
                                ALU.is_ge).then_inc(dve_chain, 1)
                dve.wait_ge(dve_chain, r * 4 + (base + 2))
                v.tensor_reduce(cnt[:, :], cmp[:, :, :], AX.X, ALU.add).then_inc(cmp_done, 1)
                dve.wait_ge(cnt_mm, r + 1)
                v.scalar_tensor_tensor(out=hit[:, :], in0=bank[7][:, 0:RATIO], scalar=float(GROUPS),
                                       in1=cand[:, :], op0=ALU.is_ge, op1=ALU.mult).then_inc(dve_chain, 1)
                dve.wait_ge(dve_chain, r * 4 + (base + 3))
                v.tensor_reduce(tau[:, :], hit[:, :], AX.X, ALU.max).then_inc(dve_chain, 1)
                dve.wait_ge(dve_chain, r * 4 + (base + 4))
            steps[0] = base + 4 * len(SHIFTS)
            link(v.tensor_scalar(gpen[:, :], gsum[:, :], tau[:, 0:1], NEVER, ALU.is_lt, ALU.mult))
            link(v.tensor_tensor(gpen[:, :], gpen[:, :], gmin[:, :], ALU.max))
            link(v.tensor_reduce(vth[:, 0:1], gpen[:, :], AX.X, ALU.min))
            v.tensor_copy(vth[0:E, 1:2], vth[E:P, 0:1])
            link(v.tensor_copy(vth[E:P, 1:2], vth[0:E, 0:1]))
            link(v.tensor_tensor(vth[:, 2:3], vth[:, 0:1], vth[:, 1:2], ALU.min))
            dve.wait_ge(probt_ready, 4)
            for s in range(2):
                rows_ = slice(E * s, E * s + E)
                v.scalar_tensor_tensor(out=gated[rows_, HT * s:HT * s + HT], in0=probt[rows_, :],
                                       scalar=vth[rows_, 2:3], in1=probt[rows_, :],
                                       op0=ALU.is_ge, op1=ALU.mult).then_inc(gate_half, 1)
            dve.wait_ge(den_mm, 1)
            link(v.tensor_scalar(rden[:, :], bank[6][:, 0:TILES], 1e-6, None, ALU.add))
            link(v.reciprocal(rden[:, :], rden[:, :]))
            xt = x_sb[:, :, :, :].rearrange("p b a d -> p (b a) d")
            dve.wait_ge(gate_dup, 32)

            def results(n):
                dve.wait_ge(back_mm, n + 2)
                dve.wait_ge(stored, (n + 1) * 16)
                for j in range(TPC):
                    t = bass.ds(n * TPC + j, 1)
                    v.scalar_tensor_tensor(out=res[:, j, :], in0=bank[5][:, P * j:P * (j + 1)],
                                           scalar=rden[:, t],
                                           in1=xt[:, t, :].rearrange("p o d -> p (o d)"),
                                           op0=ALU.mult, op1=ALU.add).then_inc(res_ready, 1)

            def hidden(n, first):
                for k in range(KT):
                    done = n * KT + k
                    dve.wait_ge(gate_mm, done + 1)
                    dve.wait_ge(silu_ready, done + 1)
                    v.scalar_tensor_tensor(out=glin[:, k % 2, :], in0=bank[2 + k % 2][:, :],
                                           scalar=cols_sb[:, V_GATE + k:V_GATE + k + 1], in1=silu[:, k % 2, :],
                                           op0=ALU.add, op1=ALU.mult).then_inc(gate_used, 1)
                    dve.wait_ge(gate_used, done + 1)
                    if not (first and k < 4):
                        dve.wait_ge(down_mm, done - 3)
                    v.tensor_tensor(hid[:, k % 4, :], glin[:, k % 2, :], gated[:, bass.ds(n * CH, CH)],
                                    ALU.mult).then_inc(hid_ready, 1)
                    if k == KT // 2 and not first:
                        results(n - 1)

            dve.sem_inc(res_ready, TPC)
            hidden(0, True)
            with dve.Fori(1, NCH) as n:
                hidden(n, False)
            results(NCH - 1)

        @block.tensor
        def _(pe):
            mm = nc.tensor.matmul

            pe.wait_ge(ld_mod, 16)
            pe.wait_ge(sc_done, 1)
            for m in range(6):
                mm(bank[0][:, B * m:B * (m + 1)], wmod_sb[:, D * m:D * (m + 1)], sc[:, :], start=True, stop=True)
            pe.wait_ge(scb_done, 1)
            for b in range(B):
                last = mm(bank[1][:, D * b:D * (b + 1)], scb[:, b, :], wmod_sb[:, 2 * D:3 * D],
                          start=True, stop=True)
            last.then_inc(mod_mm, 1)

            pe.wait_ge(ld_tabf, 16)
            pe.wait_ge(mod_read, 1)
            for a in range(AH):
                pe.wait_ge(plus_ready, a + 1)
                pe.wait_ge(minus_ready, a + 1)
                for b in range(B):
                    for par in range(2):
                        last = mm(bank[2 * b + par][:, :], fold[:, par, a, D * b:D * (b + 1)],
                                  tabf_sb[:, a, par, :], start=(a == 0), stop=(a == AH - 1))
                        if a == AH - 1:
                            last.then_inc(fwd_ready, 1)

            def project(i):
                b, par = i // 2, i % 2
                n = NRE[par]
                pe.wait_ge(xf_fixed, b + 1)
                pe.wait_ge(xf_dve, b + 1)
                for s, (done, bk, width, w) in enumerate(((q_mm, bank[par], HALF, W_Q), (k_mm, bank[2], n, W_K),
                                                          (v_mm, bank[3], n, W_V))):
                    if i == 0 and s == 1:
                        pe.wait_ge(xf_act, 2)
                    if i == 0 and s == 2:
                        pe.wait_ge(xf_dve, 2)
                    if s == 0 and i >= 2:
                        pe.wait_ge(sq_ready, i - 1)
                    if s == 1 and i >= 1:
                        pe.wait_ge(prod_ready, i)
                    if s == 2 and i >= 1:
                        pe.wait_ge(v_kept, i)
                    last = mm(bk[:, 0:width], wqkv_sb[:, s, :], xf[:, b, par, 0:width],
                              start=True, stop=(par == 1), skip_group_check=True)
                    if par == 0:
                        last = mm(bk[:, 0:1], rows_sb[0:1, w:w + D], rows_sb[0:1, W_L:W_L + 1],
                                  start=False, stop=True, skip_group_check=True)
                    last.then_inc(done, 1)

            def sum_heads(i):
                b, par = i // 2, i % 2
                n = NRE[par]
                sel = cst_sb[:, C_SEL + BH * b:C_SEL + BH * (b + 1)]
                if i == 0:
                    pe.wait_ge(xf_act, B)
                    pe.wait_ge(xf_dve, B)
                pe.wait_ge(mag_ready, i + 1)
                mm(bank[4 + par][0:BH, 0:n], sel, mag[:, par, 0:n], start=(b == 0), stop=(b == B - 1))
                pe.wait_ge(prod_ready, i + 1)
                mm(bank[6 + par][0:BH, 0:n], sel, prodqk[:, par, 0:n], start=(b == 0),
                   stop=(b == B - 1)).then_inc(head_sums, 1)

            pe.wait_ge(ld_w, 32)
            for i in range(2 * B):
                project(i)
                if i >= 1:
                    sum_heads(i - 1)
            sum_heads(2 * B - 1)

            pe.wait_ge(nsel_ready, 1)
            pe.wait_ge(attn_ready, 1)
            for i in range(2 * B):
                par, b = i // B, i % B
                n, lo = NRE[par], par * NRE[0]
                if i >= 2:
                    pe.wait_ge(ore_ready, i - 1)
                    pe.wait_ge(oim_ready, i - 1)
                exp = cst_sb[0:BH, C_EXP + P * b:C_EXP + P * (b + 1)]
                mm(bank[b % 2][:, 0:n], exp, attn[:, lo:lo + n], start=True, stop=True)
                mm(bank[2 + b % 2][:, 0:n], exp, nsel[:, lo:lo + n], start=True, stop=True).then_inc(spread, 1)

            for i in range(A):
                par = i // AH
                pe.wait_ge(ore_ready, B * (par + 1))
                pe.wait_ge(oim_ready, B * (par + 1))
                if i >= 4:
                    pe.wait_ge(y_act, i - 3)
                for b in range(B):
                    last = mm(bank[4 + i % 4][:, D * b:D * (b + 1)], of[:, b, par, P * (i % AH):P * (i % AH + 1)],
                              wob[:, b, :], start=True, stop=True)
                last.then_inc(y_mm, 1)

            pe.wait_ge(ld_tabi, 16)
            pe.wait_ge(y_fixed, 1)
            for a in range(AH):
                if a >= 2:
                    pe.wait_ge(inv_read, a - 1)
                for par, done in enumerate((inv_even, inv_odd)):
                    for i in range(AH * par, AH * (par + 1)):
                        pe.wait_ge(y_act, i + 1)
                        last = mm(bank[2 * par + a % 2][:, :], tabi_sb[:, i, P * a:P * (a + 1)], yf[:, i, :],
                                  start=(i == AH * par), stop=(i == AH * (par + 1) - 1))
                    last.then_inc(done, 1)

            def turn_in(n):
                if n >= 4:
                    pe.wait_ge(h2_act if n % 2 == 0 else h2_dve, (n - 4) // 2 + 1)
                for j in range(TPC):
                    last = nc.tensor.transpose(bank[4 + n % 4][:, P * j:P * (j + 1)],
                                               xn[:, (n % 2) * TPC + j, n // 2, :], ident)
                last.then_inc(tr_mm, 1)

            def logits(n):
                pe.wait_ge(h2_act if n % 2 == 0 else h2_dve, n // 2 + 1)
                for j in range(TPC):
                    c = ((n % 2) * TPC + j) * E
                    last = mm(bank[n // 2][:, c:c + E], h2t[:, CH * n + P * j:CH * n + P * (j + 1)], wr_sb[:, :],
                              start=True, stop=True)
                if n % 2 == 1:
                    last.then_inc(logit_mm, 1)

            pe.wait_ge(xn_ready, A)
            pe.wait_ge(inv_read, AH)
            pe.wait_ge(ld_ffn, 112)
            for n in range(NCH):
                turn_in(n)
                if n >= 2:
                    logits(n - 2)
            logits(NCH - 2)
            logits(NCH - 1)
            pe.wait_ge(prob_ready, B)
            for g in range(4):
                for j in range(4):
                    last = nc.tensor.transpose(bank[4 + g][:, P * j:P * (j + 1)],
                                               prob[:, 4 * g + j, :, :].rearrange("p h e -> p (h e)"), ident)
                last.then_inc(prob_tr, 1)

            pe.wait_ge(probt_ready, 4)
            with pe.Fori(0, len(SHIFTS)) as r:
                pe.wait_ge(cmp_done, r + 1)
                mm(bank[7][:, 0:RATIO], ones, cnt[:, :], start=True, stop=True).then_inc(cnt_mm, 1)
            pe.wait_ge(gate_half, 2)
            pe.wait_ge(gate_dup, 32)
            for t in range(TILES):
                last = mm(bank[6][:, t:t + 1], gated[0:E, P * t:P * (t + 1)], cst_sb[0:E, C_ONE:C_ONE + 1],
                          start=True, stop=True)
            last.then_inc(den_mm, 1)

            def up_gate(n, k, fresh=False):
                rhs = h2t[:, bass.ds(n * CH, CH)]
                if not fresh:
                    pe.wait_ge(silu_ready, n * KT + (k - 1))
                mm(bank[k % 2][:, :], wup_sb[:, k, :], rhs, start=True, stop=True).then_inc(up_mm, 1)
                if not fresh:
                    pe.wait_ge(gate_used, n * KT + (k - 1))
                mm(bank[2 + k % 2][:, :], wgate_sb[:, k, :], rhs, start=True, stop=True).then_inc(gate_mm, 1)

            def turn_back(n):
                pe.wait_ge(outt_ready, n + 1)
                pe.wait_ge(res_ready, (n + 1) * TPC)
                for j in range(TPC):
                    last = nc.tensor.transpose(bank[5][:, P * j:P * (j + 1)], outt[:, P * j:P * (j + 1)], ident)
                last.then_inc(back_mm, 1)

            def chunk(n, first, final):
                for k in range(KT):
                    if k < KT - 2:
                        up_gate(n, k + 2)
                    elif not final:
                        up_gate(n + 1, k + 2 - KT)
                    if k == 0:
                        if not first:
                            pe.wait_ge(outt_ready, n)
                        mm(bank[4][:, :], bdown_sb[:, :], gated[0:E, bass.ds(n * CH, CH)], start=True, stop=False)
                    pe.wait_ge(hid_ready, n * KT + (k + 1))
                    mm(bank[4][:, :], wdown_sb[:, k, :], hid[:, k % 4, :], start=False,
                       stop=(k == KT - 1)).then_inc(down_mm, 1)
                    if k == 4 and not first:
                        turn_back(n - 1)

            pe.sem_inc(back_mm, 1)
            up_gate(0, 0, True)
            up_gate(0, 1, True)
            chunk(0, True, False)
            with pe.Fori(1, NCH - 1) as n:
                chunk(n, False, False)
            chunk(NCH - 1, False, True)
            turn_back(NCH - 1)


def kernel(L0_attn_query, L0_attn_Wq, L0_attn_bq, L0_attn_Wk, L0_attn_bk, L0_attn_Wv, L0_attn_bv, L0_attn_Wo,
           L0_attn_bo, L0_ffn_Wr, L0_ffn_br, L0_ffn_Wup, L0_ffn_bup, L0_ffn_Wgate, L0_ffn_bgate, L0_ffn_Wdown,
           L0_ffn_bdown, L0_c, L0_wmod):
    import concourse.bacc as bacc
    from concourse.bass_utils import run_bass_kernel_spmd

    def arr(v):
        return np.ascontiguousarray(np.asarray(v))

    def unit_tiles(v):
        return arr(v).T.reshape(KT, P).T

    tabf, tabi = transform_tables()
    arrays = {
        "x": arr(L0_attn_query),
        "cst": constants(),
        "bits": round_bits(),
        "cols": arr(np.concatenate([arr(L0_c).T, unit_tiles(L0_ffn_bup), unit_tiles(L0_ffn_bgate)], axis=1)),
        "rows": arr(np.concatenate([arr(L0_attn_bq), arr(L0_attn_bk), arr(L0_attn_bv), arr(L0_attn_bo),
                                    np.full(1, L, np.float32)])[None, :]),
        "wmod": arr(L0_wmod),
        "wqkv": arr(np.concatenate([arr(L0_attn_Wq), arr(L0_attn_Wk), arr(L0_attn_Wv)], axis=1)),
        "wo": arr(L0_attn_Wo),
        "tabf": tabf,
        "tabi": tabi,
        "wr": arr(L0_ffn_Wr),
        "br": arr(L0_ffn_br),
        "wup": arr(arr(L0_ffn_Wup).transpose(1, 2, 0).reshape(D, E * H)),
        "wgate": arr(arr(L0_ffn_Wgate).transpose(1, 2, 0).reshape(D, E * H)),
        "wdown": arr(arr(L0_ffn_Wdown).transpose(1, 0, 2).reshape(KT, P, D).transpose(1, 0, 2).reshape(P, KT * D)),
        "bdown": arr(L0_ffn_bdown),
    }
    nc = bacc.Bacc("TRN2", target_bir_lowering=False, num_devices=1)
    args = [nc.dram_tensor(f"in_{k}", a.shape, mybir.dt.from_np(a.dtype), kind="ExternalInput").ap()
            for k, a in arrays.items()]
    out = nc.dram_tensor("out_y", (B, L, D), F32, kind="ExternalOutput").ap()
    build(nc, *args, out)
    r = run_bass_kernel_spmd(nc, [{f"in_{k}": a for k, a in arrays.items()}], core_ids=[0])
    return r.results[0]["out_y"]
```

```python
from contextlib import ExitStack

import numpy as np

import concourse.bass as bass
from concourse import mybir

ALU = mybir.AluOpType
ACT = mybir.ActivationFunctionType
F32 = mybir.dt.float32
F32R = mybir.dt.float32r
I32 = mybir.dt.int32
AX = mybir.AxisListType

P = 128
B, L, D = 4, 1024, 128
HEADS, DH = 16, 8
KTOP = 64
A = L // P
AH = A // 2
HALF = L // 2
NF = L // 2 + 1
NRE = (HALF // 2 + 1, HALF // 2)
BH = B * HEADS
E, H, G, KSEL = 64, 32, 64, 16
TOK = B * L
TILES = TOK // P
KT = E * H // P
CH = 512
NCH = TOK // CH
TPC = CH // P
PAIRS = NCH // 2
RING = 4
HT = TOK // 2
NG = HT // G
GROUPS = TOK // G * KSEL
EPS = 1e-5
RATIO = 16
SHIFTS = (27, 23, 19, 15, 11, 7, 3, 0)
NEVER = 1e30

C_ID, C_ONE, C_SGN, C_SEL, C_EXP = 0, P, 2 * P, 2 * P + 1, 2 * P + 1 + B * BH
C_ROW = C_EXP + B * P
C_ALL = C_ROW + NCH * NCH
V_C, V_UP, V_GATE, V_ALL = 0, B, B + KT, B + 2 * KT
W_Q, W_K, W_V, W_O, W_L, W_ALL = 0, P, 2 * P, 3 * P, 4 * P, 4 * P + 1


def transform_tables():
    t = np.arange(HALF)[:, None]
    fwd, inv = [], []
    for par in range(2):
        fre = 2 * np.arange(NRE[par])[None, :] + par
        fim = fre[:, 1:HALF // 2] if par == 0 else fre
        are, aim = 2 * np.pi * ((t * fre) % L) / L, 2 * np.pi * ((t * fim) % L) / L
        fwd.append(np.concatenate([np.cos(are), -np.sin(aim)], axis=1))
        weight = np.where((fre == 0) | (fre == HALF), 1.0, 2.0)
        inv.append(np.concatenate([weight * np.cos(are), -2.0 * np.sin(aim)], axis=1).T / L)
    fwd = np.stack(fwd, axis=1).reshape(AH, P, 2, HALF).transpose(1, 0, 2, 3)
    inv = np.concatenate(inv, axis=0).reshape(A, P, HALF).transpose(1, 0, 2)
    return (np.ascontiguousarray(fwd.reshape(P, -1), dtype=np.float32),
            np.ascontiguousarray(inv.reshape(P, -1), dtype=np.float32))


def constants():
    c = np.zeros((P, C_ALL), np.float32)
    c[:, C_ID:C_ID + P] = np.eye(P)
    c[:, C_ONE:C_ONE + P] = 1.0
    c[:, C_SGN] = np.where(np.arange(P) < E, 1.0, -1.0)
    for b in range(B):
        for ch in range(D):
            row = b * HEADS + ch // DH
            c[ch, C_SEL + b * BH + row] = 1.0
            c[row, C_EXP + b * P + ch] = 1.0
    for n in range(NCH):
        c[:, C_ROW + n * NCH + n] = 1.0
    return c


def round_bits():
    bits = np.zeros((len(SHIFTS), RATIO), np.int32)
    for r, s in enumerate(SHIFTS):
        width = (SHIFTS[r - 1] if r else 31) - s
        bits[r] = np.minimum(np.arange(RATIO), 2 ** width - 1).astype(np.int32) << s
    return np.ascontiguousarray(np.broadcast_to(bits.reshape(1, -1), (P, bits.size)))


def build(nc, x, cst, bits, cols, rows, wmod, wqkv, wo, tabf, tabi, wr, br, wup, wgate, wdown, bdown, out):
    with ExitStack() as ctx:
        def sb(name, shape, dt=F32):
            return ctx.enter_context(nc.sbuf_tensor(name, shape, dt))

        def sem(name):
            return ctx.enter_context(nc.semaphore(name))

        bank = [ctx.enter_context(nc.psum_tensor(f"bank{i}", [P, 512], F32)) for i in range(8)]

        base = -(-nc.sbuf_base // 32) * 32
        size = 4 * TOK
        top = [base]

        def region(nbytes):
            at = top[0]
            top[0] += -(-nbytes // 32) * 32
            return [at, at + nbytes]

        def put(reg, name, shape, dt=F32):
            at = reg[0]
            reg[0] += -(-int(np.prod(shape[1:])) * 4 // 32) * 32
            assert reg[0] <= reg[1], name
            return nc.alloc_sbuf_tensor_at(name, shape, dt, offset=at)

        def stage(reg):
            return list(reg)

        def sb(name, shape, dt=F32):
            return put(region(-(-int(np.prod(shape[1:])) * 4 // 32) * 32), name, shape, dt)

        r_xn, r_fold, r_table, r_tabi, r_freq, r_q, r_of, r_yf = (region(size) for _i in range(8))
        r_vf = region(-(-4 * B * NF // 32) * 32)
        r_att = region(4 * (6 * D + 4 * D + 3 * B * D))

        x_sb = sb("x_sb", [P, B, A, D])
        xn = put(stage(r_xn), "xn", [P, A, B, D])
        fold = put(stage(r_fold), "fold", [P, 2, AH, B * D])
        tabf_sb = put(stage(r_table), "tabf_sb", [P, AH, 2, HALF])
        tabi_sb = put(stage(r_tabi), "tabi_sb", [P, A, HALF])
        xf = put(stage(r_freq), "xf", [P, B, 2, HALF])
        qf = put(stage(r_q), "qf", [P, B, 2, HALF])
        vf = put(stage(r_vf), "vf", [P, B, NF])
        s = stage(r_of)
        w_raw = [put(s, f"w_raw{i}", [P, KT, P]) for i in range(2)]
        of = put(stage(r_of), "of", [P, B, 2, HALF])
        s = stage(r_yf)
        sq = put(s, "sq", [P, 2, HALF])
        e2 = put(s, "e2", [P, 2, NRE[0]])
        mag = put(s, "mag", [P, 2, NRE[0]])
        prodqk = put(s, "prodqk", [P, 2, NRE[0]])
        s = stage(r_yf)
        scb = put(s, "scb", [P, B, P])
        gsign = put(s, "gsign", [P, B * D])
        gabs = put(s, "gabs", [P, B * D])
        yf = put(stage(r_yf), "yf", [P, A, B * D])
        s = stage(r_fold)
        energy = put(s, "energy", [BH, NF])
        nsel = put(s, "nsel", [BH, NF])
        masked = put(s, "masked", [BH, NF])
        attn = put(s, "attn", [BH, NF])
        av = put(s, "av", [P, NRE[0]])
        s = stage(r_att)
        wmod_sb = put(s, "wmod_sb", [P, 6 * D])
        wqkv_sb = put(s, "wqkv_sb", [P, 3, D])
        wo_sb = put(s, "wo_sb", [P, D])
        gval = put(s, "gval", [P, B * D])
        wob = put(s, "wob", [P, B, D])
        bol = put(s, "bol", [1, B * D])
        tsum = put(stage(r_q), "tsum", [P, 2, B * D])
        h2t = put(stage(r_fold), "h2t", [P, TOK])
        h2hi = put(stage(r_of), "h2hi", [P, TOK], F32R)
        h2lo = put(stage(r_yf), "h2lo", [P, TOK], F32R)
        logit = put(stage(r_vf), "logit", [P, 2, 8, E])
        wdown_sb = put(stage(r_vf), "wdown_sb", [P, KT, D])
        s = stage(r_freq)
        prob = put(s, "prob", [P, HT // P, 2, E])
        probt = put(s, "probt", [P, HT])
        keys = put(stage(r_table), "keys", [P, 2, HT])
        gated = put(stage(r_q), "gated", [P, TOK])
        s = stage(r_fold)
        swapped = put(s, "swapped", [P, HT])
        cmp = put(s, "cmp", [P, RATIO, NG])
        held = put(stage(r_xn), "held", [P, RING, 2, CH])
        back = put(stage(r_freq), "back", [P, RING, 2, CH])
        s = stage(r_xn)
        silu = put(s, "silu", [P, 2, CH])
        glin_f = put(s, "glin_f", [P, CH])
        glin_s = put(s, "glin_s", [P, CH])
        hid_f = put(s, "hid_f", [P, 2, CH])
        outt = put(s, "outt", [P, 2, CH])
        s = stage(r_tabi)
        hid_hi = put(s, "hid_hi", [P, RING, CH], F32R)
        hid_lo = put(s, "hid_lo", [P, RING, CH], F32R)
        s = stage(r_fold)
        hid_s = put(s, "hid_s", [P, RING, CH])
        res = put(s, "res", [P, 2, TPC, D])
        den_sb = put(s, "den_sb", [NCH, CH])

        cst_sb = sb("cst_sb", [P, C_ALL])
        bits_sb = sb("bits_sb", [P, len(SHIFTS) * RATIO], I32)
        cols_sb = sb("cols_sb", [P, V_ALL])
        rows_sb = sb("rows_sb", [1, W_ALL])
        wr_sb = sb("wr_sb", [P, E])
        br_sb = sb("br_sb", [P, E])
        wup_hi = sb("wup_hi", [P, KT, P], F32R)
        wup_lo = sb("wup_lo", [P, KT, P], F32R)
        wgate_hi = sb("wgate_hi", [P, KT, P], F32R)
        wgate_lo = sb("wgate_lo", [P, KT, P], F32R)
        wdown_hi = put(stage(r_table), "wdown_hi", [P, KT, D], F32R)
        wdown_lo = put(stage(r_att), "wdown_lo", [P, KT, D], F32R)
        bdown_sb = sb("bdown_sb", [E, D])
        sc = sb("sc", [P, B])
        mods = sb("mods", [P, 6, B])
        camod = sb("camod", [P, 2, B])
        sal = sb("sal", [P, B])
        gb8 = sb("gb8", [P, B, 2])
        stats = sb("stats", [P, B, A, 6])
        lns = sb("lns", [P, 7, B, 2])
        acc = sb("acc", [P, 2, B, 2])
        qmean = sb("qmean", [P, 2, B])
        top8 = sb("top8", [BH, 8])
        hstat = sb("hstat", [BH, 4])
        sm = sb("sm", [P, 3, 8])
        gsum = sb("gsum", [P, NG])
        gmin = sb("gmin", [P, NG])
        cand = sb("cand", [P, RATIO])
        cnt = sb("cnt", [P, RATIO])
        hit = sb("hit", [P, RATIO])
        tau = sb("tau", [P, 1])
        gpen = sb("gpen", [P, NG])
        vth = sb("vth", [P, 3])
        rden = sb("rden", [P, TPC, NCH])
        assert top[0] <= nc.sbuf_usable_end, (top[0], nc.sbuf_usable_end)

        ident = cst_sb[:, C_ID:C_ID + P]
        ones = cst_sb[:, C_ONE:C_ONE + P]
        gb_chunk = gb8[:, :, :].rearrange("p b c -> p (b c)")

        ld_c = sem("ld_c")
        ld_x = [sem(f"ld_x{a}") for a in range(AH)]
        ld_mod = sem("ld_mod")
        ld_tabf = sem("ld_tabf")
        ld_w = sem("ld_w")
        ld_tabi = sem("ld_tabi")
        ld_ffn = sem("ld_ffn")
        sc_done = sem("sc_done")
        scb_done = sem("scb_done")
        mod_mm = sem("mod_mm")
        mod_read = sem("mod_read")
        var_ready = sem("var_ready")
        std_ready = sem("std_ready")
        xn_ready = sem("xn_ready")
        plus_ready = sem("plus_ready")
        minus_ready = sem("minus_ready")
        fwd_ready = sem("fwd_ready")
        xf_act = sem("xf_act")
        xf_dve = sem("xf_dve")
        xf_fixed = sem("xf_fixed")
        q_mm = sem("q_mm")
        k_mm = sem("k_mm")
        v_mm = sem("v_mm")
        q_kept = sem("q_kept")
        sq_ready = sem("sq_ready")
        e2_ready = sem("e2_ready")
        mag_ready = sem("mag_ready")
        prod_ready = sem("prod_ready")
        v_kept = sem("v_kept")
        head_sums = sem("head_sums")
        en_read = sem("en_read")
        smax_ready = sem("smax_ready")
        exp_ready = sem("exp_ready")
        attn_ready = sem("attn_ready")
        nsel_ready = sem("nsel_ready")
        qmean_ready = sem("qmean_ready")
        spread = sem("spread")
        oim_ready = sem("oim_ready")
        ore_ready = sem("ore_ready")
        y_mm = sem("y_mm")
        y_act = sem("y_act")
        y_fixed = sem("y_fixed")
        inv_even = sem("inv_even")
        inv_odd = sem("inv_odd")
        inv_read = sem("inv_read")
        tr_mm = sem("tr_mm")
        h2_act = sem("h2_act")
        h2_dve = sem("h2_dve")
        logit_mm = sem("logit_mm")
        logit_read = sem("logit_read")
        centred = sem("centred")
        rexp = sem("rexp")
        prob_ready = sem("prob_ready")
        prob_tr = sem("prob_tr")
        probt_ready = sem("probt_ready")
        cmp_done = sem("cmp_done")
        cnt_mm = sem("cnt_mm")
        dve_chain = sem("dve_chain")
        raw_loaded = [sem(f"raw_loaded{i}") for i in range(3)]
        raw_hi = sem("raw_hi")
        raw_lo = sem("raw_lo")
        h2_hi = sem("h2_hi")
        h2_lo = sem("h2_lo")
        scores_dup = sem("scores_dup")
        keys_made = sem("keys_made")
        groups_summed = sem("groups_summed")
        pre_up = sem("pre_up")
        pre_gate = sem("pre_gate")
        silu_held = sem("silu_held")
        gate_held = sem("gate_held")
        put_off = [sem(f"put_off{i}") for i in range(RING)]
        fetched = [sem(f"fetched{i}") for i in range(RING)]
        fetch_used = sem("fetch_used")
        up_mm = sem("up_mm")
        gate_mm = sem("gate_mm")
        silu_ready = sem("silu_ready")
        gate_used = sem("gate_used")
        kept_ready = sem("kept_ready")
        hid_f_ready = sem("hid_f_ready")
        hid_s_ready = sem("hid_s_ready")
        hi_ready = sem("hi_ready")
        lo_dve = sem("lo_dve")
        lo_pool = sem("lo_pool")
        down_f = sem("down_f")
        down_s = sem("down_s")
        out_f = sem("out_f")
        out_s = sem("out_s")
        turned_f = sem("turned_f")
        turned_s = sem("turned_s")
        res_f = sem("res_f")
        res_s = sem("res_s")
        stored_f = sem("stored_f")
        stored_s = sem("stored_s")
        den_rows = sem("den_rows")
        den_kept = sem("den_kept")
        den_turned = sem("den_turned")

        spill = nc.dram_tensor("spill", [PAIRS * KT, P, 2, CH], F32, kind="Internal").ap()

        block = ctx.enter_context(nc.Block())

        def pair(view, a):
            return view[:, :, a:a + AH + 1:AH]

        @block.sync
        def _(sp):
            xv = x.rearrange("b (a p) d -> a p b d", p=P)
            for a in range(AH):
                for t in (a, a + AH):
                    sp.dma_start(x_sb[:, :, t, :], xv[t]).then_inc(ld_x[a], 16)
            sp.dma_start(wqkv_sb[:, :, :], wqkv.rearrange("d (s n) -> d s n", s=3)).then_inc(ld_w, 16)
            sp.dma_start(wo_sb[:, :], wo).then_inc(ld_w, 16)
            sp.dma_start(tabi_sb[:, :, :], tabi.rearrange("p (a n) -> p a n", a=A)).then_inc(ld_tabi, 16)
            sp.dma_start(wr_sb[:, :], wr).then_inc(ld_ffn, 16)
            sp.dma_start(br_sb[:, :], br.partition_broadcast(P)).then_inc(ld_ffn, 16)
            sp.dma_start(bdown_sb[:, :], bdown).then_inc(ld_ffn, 16)
            sp.dma_start(bits_sb[:, :], bits).then_inc(ld_ffn, 16)
            for i, w in enumerate((wup, wgate)):
                sp.dma_start(w_raw[i][:, :, :], w.rearrange("d (k n) -> d k n", k=KT)).then_inc(raw_loaded[i], 16)
            for i in range(RING):
                sp.sem_inc(put_off[i], 16)
            sp.sem_inc(stored_s, 16)
            sp.sem_inc(stored_f, 16)
            sp.wait_ge(prob_ready, B)
            sp.dma_start(wdown_sb[:, :, :], wdown.rearrange("p (k n) -> p k n", k=KT)).then_inc(raw_loaded[2], 16)
            sp.wait_ge(probt_ready, 4)
            for half in range(2):
                for unit in range(2):
                    sp.dma_start(gated[E * unit:E * unit + E, HT * half:HT * half + HT],
                                 probt[E * half:E * half + E, :]).then_inc(scores_dup, 16)
            with sp.Fori(0, PAIRS) as n:
                for k in range(KT):
                    sp.wait_ge(silu_held, n * KT + (k + 3))
                    sp.wait_ge(gate_held, n * KT + (k + 3))
                    sp.dma_start(spill[bass.ds(n * KT + k, 1)].rearrange("o p s c -> (o p) s c"),
                                 held[:, k % RING]).then_inc(put_off[k % RING], 16)
            for i in range(RING):
                sp.wait_ge(put_off[i], 16 * (PAIRS * KT // RING + 1))
            sp.wait_ge(scores_dup, 64)
            sp.wait_ge(keys_made, 1)
            ov = out.rearrange("b (c j p) d -> (b c) p j d", j=TPC, p=P)

            def fetch(n, k):
                sp.wait_ge(fetch_used, n * KT + (k + 1))
                sp.dma_start(back[:, k % RING],
                             spill[bass.ds(n * KT + k, 1)].rearrange("o p s c -> (o p) s c")
                             ).then_inc(fetched[k % RING], 16)

            def store(n):
                sp.wait_ge(res_s, (n + 2) * TPC)
                sp.dma_start(ov[bass.ds(n, 1)].rearrange("o p j d -> (o p) j d"), res[:, 0]).then_inc(stored_s, 16)
                sp.wait_ge(res_f, (n + 2) * TPC)
                sp.dma_start(ov[bass.ds(n + PAIRS, 1)].rearrange("o p j d -> (o p) j d"), res[:, 1]
                             ).then_inc(stored_f, 16)

            for k in range(KT):
                fetch(0, k)
            with sp.Fori(1, PAIRS) as n:
                for k in range(KT):
                    fetch(n, k)
                    if k == 13:
                        store(n - 1)
            store(PAIRS - 1)
            sp.wait_ge(stored_s, 16 * (PAIRS + 1))
            sp.wait_ge(stored_f, 16 * (PAIRS + 1))

        @block.gpsimd
        def _(pool):
            for a in range(AH):
                pool.wait_ge(xn_ready, a + 1)
                nc.gpsimd.tensor_tensor(fold[:, 1, a, :].rearrange("p (b d) -> p b d", b=B),
                                        xn[:, a], xn[:, a + AH], ALU.subtract).then_inc(minus_ready, 1)
            def split(i, w, hi, lo):
                pool.wait_ge(raw_loaded[i], 16)
                nc.gpsimd.tensor_copy(hi[:, :, :], w[:, :, :]).then_inc(raw_hi, 1)
                pool.wait_ge(raw_hi, i + 1)
                nc.gpsimd.tensor_tensor(lo[:, :, :], w[:, :, :], hi[:, :, :].bitcast(F32),
                                        ALU.subtract).then_inc(raw_lo, 1)

            split(0, w_raw[0], wup_hi, wup_lo)
            split(1, w_raw[1], wgate_hi, wgate_lo)
            for n in range(NCH):
                pool.wait_ge(h2_hi, n + 1)
                c = slice(CH * n, CH * (n + 1))
                nc.gpsimd.tensor_tensor(h2lo[:, c], h2t[:, c], h2hi[:, c].bitcast(F32),
                                        ALU.subtract).then_inc(h2_lo, 1)
            pool.wait_ge(groups_summed, 1)
            split(2, wdown_sb, wdown_hi, wdown_lo)

            def lower(n, k):
                pool.wait_ge(hi_ready, n * KT + (k + 1))
                pool.wait_ge(down_f, n * KT + (k + 1))
                nc.gpsimd.tensor_tensor(hid_lo[:, k % RING], hid_f[:, k % 2], hid_hi[:, k % RING].bitcast(F32),
                                        ALU.subtract).then_inc(lo_pool, 1)

            with pool.Fori(0, PAIRS) as n:
                for k in range(1, KT, 2):
                    lower(n, k)

        @block.scalar
        def _(act):
            act.dma_start(cols_sb[:, :], cols).then_inc(ld_c, 16)
            act.dma_start(rows_sb[:, :], rows).then_inc(ld_c, 16)
            act.dma_start(wmod_sb[:, :], wmod).then_inc(ld_mod, 16)
            act.dma_start(cst_sb[:, :], cst).then_inc(ld_c, 16)
            act.dma_start(tabf_sb[:, :, :, :], tabf.rearrange("p (a s c) -> p a s c", a=AH, s=2)).then_inc(ld_tabf, 16)
            act.wait_ge(ld_c, 48)
            nc.scalar.activation(sc[:, :], cols_sb[:, V_C:V_C + B], ACT.Silu).then_inc(sc_done, 1)

            def std(n):
                act.wait_ge(var_ready, n + 1)
                nc.scalar.activation(lns[:, 5], lns[:, 4], ACT.Sqrt).then_inc(std_ready, 1)

            for a in range(AH):
                std(a)
            for b in range(B):
                act.wait_ge(fwd_ready, 2 * b + 1)
                act.wait_ge(mod_read, 2)
                nc.scalar.activation(xf[:, b, 0, :], bank[2 * b][:, :], ACT.Copy,
                                     scale=camod[:, 0, b:b + 1]).then_inc(xf_act, 1)

            def magnitude(i):
                act.wait_ge(e2_ready, i + 1)
                if i >= 2:
                    act.wait_ge(head_sums, i - 1)
                par = i % 2
                nc.scalar.activation(mag[:, par, 0:NRE[par]], e2[:, par, 0:NRE[par]],
                                     ACT.Sqrt).then_inc(mag_ready, 1)

            for i in range(2 * B):
                b, par = i // 2, i % 2
                n = NRE[par]
                act.wait_ge(q_mm, i + 1)
                nc.scalar.activation(qf[:, b, par, 0:n], bank[par][:, 0:n], ACT.Copy,
                                     accum_out=acc[:, 0, b, par:par + 1])
                nc.scalar.activation(qf[:, b, par, n:HALF], bank[par][:, n:HALF], ACT.Copy,
                                     accum_out=acc[:, 1, b, par:par + 1]).then_inc(q_kept, 1)
                if i >= 2:
                    act.wait_ge(e2_ready, i - 1)
                nc.scalar.activation(sq[:, par, :], bank[par][:, :], ACT.Square).then_inc(sq_ready, 1)
                if i >= 1:
                    magnitude(i - 1)
            magnitude(2 * B - 1)
            act.wait_ge(smax_ready, 1)
            nc.scalar.activation(attn[:, :], masked[:, :], ACT.Exp, bias=hstat[:, 1:2],
                                 scale=1.0 / (DH ** 0.5 + 1e-8), accum_out=hstat[:, 2:3]).then_inc(exp_ready, 1)
            act.wait_ge(qmean_ready, 1)
            act.wait_ge(raw_lo, 2)
            for i in range(2 * B):
                par, b = i // B, i % B
                act.wait_ge(spread, i + 1)
                lo = 1 - par
                nc.scalar.activation(of[:, b, par, NRE[par]:HALF], bank[2 + b % 2][:, lo:HALF // 2],
                                     ACT.Copy, scale=qmean[:, 1, b:b + 1]).then_inc(oim_ready, 1)
            for i in range(A):
                act.wait_ge(y_mm, i + 1)
                nc.scalar.copy(yf[:, i, :], bank[4 + i % 4][:, :]).then_inc(y_act, 1)
            for a in range(AH):
                std(AH + a)
            for n in range(0, NCH, 2):
                b = n // 2
                act.wait_ge(tr_mm, n + 1)
                nc.scalar.activation(h2t[:, CH * n:CH * (n + 1)], bank[4 + n % 4][:, :], ACT.Identity,
                                     scale=camod[:, 1, b:b + 1], bias=mods[:, 3, b:b + 1]).then_inc(h2_act, 1)
            for n in range(NCH):
                act.wait_ge(h2_act if n % 2 == 0 else h2_dve, n // 2 + 1)
                nc.scalar.activation(h2hi[:, CH * n:CH * (n + 1)], h2t[:, CH * n:CH * (n + 1)],
                                     ACT.Copy).then_inc(h2_hi, 1)
                if n % 2 == 1:
                    g = n // 2
                    act.wait_ge(centred, g + 1)
                    nc.scalar.activation(logit[:, g % 2], logit[:, g % 2], ACT.Exp).then_inc(rexp, 1)
            for g in range(4):
                act.wait_ge(prob_tr, g + 1)
                nc.scalar.copy(probt[:, CH * g:CH * (g + 1)], bank[4 + g][:, :]).then_inc(probt_ready, 1)

            act.sem_inc(silu_held, 2)
            act.sem_inc(gate_held, 2)
            with act.Fori(0, PAIRS) as n:
                for k in range(KT):
                    act.wait_ge(pre_up, n * KT + (k + 1))
                    act.wait_ge(put_off[k % RING], n * (16 * KT // RING) + 16 * (k // RING + 1))
                    nc.scalar.activation(held[:, k % RING, 0], bank[k % 2][:, :], ACT.Silu,
                                         bias=cols_sb[:, V_UP + k:V_UP + k + 1]).then_inc(silu_held, 1)
                    act.wait_ge(pre_gate, n * KT + (k + 1))
                    nc.scalar.activation(held[:, k % RING, 1], bank[2 + k % 2][:, :], ACT.Identity,
                                         bias=cols_sb[:, V_GATE + k:V_GATE + k + 1]).then_inc(gate_held, 1)

            def shift_out(n):
                for s, (c, done, read, ready) in enumerate(((n + PAIRS, down_f, turned_f, out_f),
                                                            (n, down_s, turned_s, out_s))):
                    act.wait_ge(done, (n + 1) * KT + (RING if s == 0 else 0))
                    act.wait_ge(read, n + 1)
                    nc.scalar.activation(outt[:, s], bank[4 + s][:, :], ACT.Copy,
                                         scale=gb_chunk[:, bass.ds(c, 1)]).then_inc(ready, 1)

            def silus(n, first):
                for k in range(KT):
                    if k == 2 and not first:
                        shift_out(n - 1)
                    act.wait_ge(up_mm, n * KT + (k + 1))
                    if not (first and k < 2):
                        act.wait_ge(gate_used, n * KT + (k - 1))
                    nc.scalar.activation(silu[:, k % 2, :], bank[k % 2][:, :], ACT.Silu,
                                         bias=cols_sb[:, V_UP + k:V_UP + k + 1]).then_inc(silu_ready, 1)
                    act.wait_ge(hid_f_ready, n * KT + (k + 1))
                    act.wait_ge(down_f, n * KT + (k + 1))
                    nc.scalar.activation(hid_hi[:, k % RING], hid_f[:, k % 2], ACT.Copy).then_inc(hi_ready, 1)

            for i in range(RING):
                act.wait_ge(put_off[i], 16 * (PAIRS * KT // RING + 1))
            silus(0, True)
            with act.Fori(1, PAIRS) as n:
                silus(n, False)
            shift_out(PAIRS - 1)

        @block.vector
        def _(dve):
            steps = [0]

            def link(ins):
                steps[0] += 1
                ins.then_inc(dve_chain, 1)
                dve.wait_ge(dve_chain, steps[0])

            v = nc.vector
            dve.sem_inc(fetch_used, RING)
            dve.sem_inc(res_f, TPC)
            dve.sem_inc(res_s, TPC)
            dve.wait_ge(sc_done, 1)
            v.tensor_copy(scb[:, :, :], sc[:, :].unsqueeze(2).broadcast_to([P, B, P])).then_inc(scb_done, 1)

            def ln_stats(a):
                for b in range(B):
                    for t in (a, a + AH):
                        ins = v.bn_stats(stats[:, b, t, :], x_sb[:, b, t, :])
                link(ins)
                st = pair(stats, a)
                me, m2e, mo, m2o = st[:, :, :, 1], st[:, :, :, 2], st[:, :, :, 4], st[:, :, :, 5]
                v.tensor_tensor(lns[:, 0], me, mo, ALU.add)
                v.tensor_tensor(lns[:, 1], me, mo, ALU.subtract)
                link(v.tensor_tensor(lns[:, 2], m2e, m2o, ALU.add))
                v.tensor_scalar(lns[:, 6], lns[:, 0], 0.5, None, ALU.mult)
                v.scalar_tensor_tensor(out=lns[:, 3], in0=lns[:, 1], scalar=0.25, in1=lns[:, 1],
                                       op0=ALU.mult, op1=ALU.mult)
                link(v.tensor_scalar(lns[:, 2], lns[:, 2], 1.0 / D, EPS, ALU.mult, ALU.add))
                v.tensor_tensor(lns[:, 4], lns[:, 3], lns[:, 2], ALU.add).then_inc(var_ready, 1)

            def ln_apply(n, a):
                dve.wait_ge(std_ready, n + 1)
                link(v.reciprocal(lns[:, 5], lns[:, 5]))
                for b in range(B):
                    for s, t in enumerate((a, a + AH)):
                        ins = v.tensor_scalar(xn[:, t, b, :], x_sb[:, b, t, :], lns[:, 6, b, s:s + 1],
                                              lns[:, 5, b, s:s + 1], ALU.subtract, ALU.mult)
                ins.then_inc(xn_ready, 1)

            def modulation():
                dve.wait_ge(mod_mm, 1)
                link(v.tensor_copy(mods[:, :, :], bank[0][:, 0:6 * B].rearrange("p (m b) -> p m b", b=B)))
                v.tensor_scalar(camod[:, 0, :], mods[:, 1, :], 1.0, None, ALU.add)
                v.tensor_scalar(camod[:, 1, :], mods[:, 4, :], 1.0, None, ALU.add)
                v.tensor_scalar(sal[:, :], mods[:, 0, :], float(L), None, ALU.mult)
                link(v.tensor_copy(gval[:, :], bank[1][:, :]))
                dve.sem_inc(mod_read, 1)
                link(away_from_zero(gb8[:, :, 0], mods[:, 5, :], B))
                v.tensor_copy(gb8[:, :, 1], gb8[:, :, 0])
                away_from_zero(gval[:, :], gval[:, :], B * D).then_inc(mod_read, 1)

            def away_from_zero(out_, g, n):
                link(v.tensor_scalar(gsign[:, 0:n], g, 0.0, None, ALU.is_ge))
                v.tensor_scalar(gsign[:, 0:n], gsign[:, 0:n], 2.0, -1.0, ALU.mult, ALU.add)
                link(v.scalar_tensor_tensor(out=gabs[:, 0:n], in0=g, scalar=-1.0, in1=g, op0=ALU.mult, op1=ALU.max))
                return v.scalar_tensor_tensor(out=out_, in0=gabs[:, 0:n], scalar=0.25, in1=gsign[:, 0:n],
                                              op0=ALU.max, op1=ALU.mult)

            for a in range(AH):
                dve.wait_ge(ld_x[a], 32)
                ln_stats(a)
                if a == 0:
                    modulation()
                ln_apply(a, a)
                dve.wait_ge(xn_ready, a + 1)
                v.tensor_tensor(fold[:, 0, a, :].rearrange("p (b d) -> p b d", b=B),
                                xn[:, a], xn[:, a + AH], ALU.add).then_inc(plus_ready, 1)
            dve.wait_ge(ld_w, 32)
            dve.wait_ge(mod_read, 2)
            v.tensor_tensor(wob[:, :, :], wo_sb[:, :].unsqueeze(1).broadcast_to([P, B, D]),
                            gval[:, :].rearrange("p (b d) -> p b d", b=B), ALU.mult)
            link(v.scalar_tensor_tensor(out=bol[:, :].rearrange("p (b d) -> p b d", b=B),
                                        in0=rows_sb[0:1, W_O:W_O + D].unsqueeze(1).broadcast_to([1, B, D]),
                                        scalar=float(L), in1=gval[0:1, :].rearrange("p (b d) -> p b d", b=B),
                                        op0=ALU.mult, op1=ALU.mult))
            for b in range(B):
                dve.wait_ge(fwd_ready, 2 * b + 2)
                v.tensor_scalar(xf[:, b, 1, :], bank[2 * b + 1][:, :], camod[:, 0, b:b + 1], None,
                                ALU.mult).then_inc(xf_dve, 1)
                dve.wait_ge(xf_act, b + 1)
                v.tensor_tensor(xf[:, b, 0, 0:1], xf[:, b, 0, 0:1], sal[:, b:b + 1],
                                ALU.add).then_inc(xf_fixed, 1)
            for i in range(2 * B):
                b, par = i // 2, i % 2
                n = NRE[par]
                if i >= 2:
                    dve.wait_ge(head_sums, i - 1)
                dve.wait_ge(k_mm, i + 1)
                dve.wait_ge(q_kept, i + 1)
                v.tensor_tensor(prodqk[:, par, 0:n], bank[2][:, 0:n], qf[:, b, par, 0:n],
                                ALU.mult).then_inc(prod_ready, 1)
                dve.wait_ge(v_mm, i + 1)
                v.tensor_copy(vf[:, b, par * NRE[0]:par * NRE[0] + n], bank[3][:, 0:n]).then_inc(v_kept, 1)
                dve.wait_ge(sq_ready, i + 1)
                if i >= 2:
                    dve.wait_ge(mag_ready, i - 1)
                if par == 0:
                    v.tensor_copy(e2[:, 0, 0:HALF // 2 + 1:HALF // 2], sq[:, 0, 0:HALF // 2 + 1:HALF // 2])
                    v.tensor_tensor(e2[:, 0, 1:HALF // 2], sq[:, 0, 1:HALF // 2], sq[:, 0, n:HALF],
                                    ALU.add).then_inc(e2_ready, 1)
                else:
                    v.tensor_tensor(e2[:, 1, 0:n], sq[:, 1, 0:n], sq[:, 1, n:HALF],
                                    ALU.add).then_inc(e2_ready, 1)
            v.tensor_tensor(qmean[:, :, :], acc[:, :, :, 0], acc[:, :, :, 1], ALU.add)
            dve.wait_ge(head_sums, 2 * B)
            link(v.tensor_copy(energy[:, 0:NRE[0]], bank[4][0:BH, 0:NRE[0]]))
            link(v.tensor_copy(energy[:, NRE[0]:NF], bank[5][0:BH, 0:NRE[1]]))
            v.tensor_scalar(qmean[:, :, :], qmean[:, :, :], 1.0 / NF, None, ALU.mult).then_inc(qmean_ready, 1)
            for _i in range(KTOP // 8):
                link(v.max(top8[:, :], energy[:, :]))
                link(v.match_replace(energy[:, :], top8[:, :], energy[:, :], -1.0))
            v.tensor_scalar(nsel[:, :], energy[:, :], 0.0, None, ALU.is_ge).then_inc(nsel_ready, 1)
            dve.wait_ge(nsel_ready, 1)
            for s, (lo, hi) in enumerate(((0, NRE[0]), (NRE[0], NF))):
                ins = v.scalar_tensor_tensor(out=masked[:, lo:hi], in0=nsel[:, lo:hi], scalar=-NEVER,
                                             in1=bank[6 + s][0:BH, 0:hi - lo], op0=ALU.mult, op1=ALU.add)
            ins.then_inc(en_read, 1)
            dve.wait_ge(en_read, 1)
            link(v.tensor_reduce(hstat[:, 0:1], masked[:, :], AX.X, ALU.max))
            v.tensor_scalar(hstat[:, 1:2], hstat[:, 0:1], -1.0 / (DH ** 0.5 + 1e-8), None,
                            ALU.mult).then_inc(smax_ready, 1)
            dve.wait_ge(exp_ready, 1)
            link(v.reciprocal(hstat[:, 3:4], hstat[:, 2:3]))
            v.tensor_scalar(attn[:, :], attn[:, :], hstat[:, 3:4], None, ALU.mult).then_inc(attn_ready, 1)
            dve.wait_ge(raw_lo, 2)
            for i in range(2 * B):
                par, b = i // B, i % B
                n = NRE[par]
                dve.wait_ge(spread, i + 1)
                link(v.tensor_tensor(av[:, 0:n], bank[b % 2][:, 0:n],
                                     vf[:, b, par * NRE[0]:par * NRE[0] + n], ALU.mult))
                dve.wait_ge(oim_ready, i + 1)
                v.scalar_tensor_tensor(out=of[:, b, par, 0:n], in0=bank[2 + b % 2][:, 0:n],
                                       scalar=qmean[:, 0, b:b + 1], in1=av[:, 0:n],
                                       op0=ALU.mult, op1=ALU.add).then_inc(ore_ready, 1)
                dve.wait_ge(ore_ready, i + 1)
            dve.wait_ge(y_act, 1)
            v.tensor_tensor(yf[0:1, 0, :], yf[0:1, 0, :], bol[:, :], ALU.add).then_inc(y_fixed, 1)

            for a in range(AH):
                dve.wait_ge(inv_even, a + 1)
                ev = bank[a % 2][:, :].rearrange("p (b d) -> p b d", b=B)
                od = bank[2 + a % 2][:, :].rearrange("p (b d) -> p b d", b=B)
                ts = [tsum[:, s, :].rearrange("p (b d) -> p b d", b=B) for s in range(2)]
                v.tensor_tensor(ts[0], x_sb[:, :, a, :], ev, ALU.add)
                link(v.tensor_tensor(ts[1], x_sb[:, :, a + AH, :], ev, ALU.add))
                dve.wait_ge(inv_odd, a + 1)
                v.tensor_tensor(x_sb[:, :, a, :], ts[0], od, ALU.add)
                v.tensor_tensor(x_sb[:, :, a + AH, :], ts[1], od, ALU.subtract).then_inc(inv_read, 1)
                dve.wait_ge(inv_read, a + 1)
                ln_stats(a)
                ln_apply(AH + a, a)
            for n in range(1, NCH, 2):
                dve.wait_ge(tr_mm, n + 1)
                v.tensor_scalar(h2t[:, CH * n:CH * (n + 1)], bank[4 + n % 4][:, :], camod[:, 1, n // 2:n // 2 + 1],
                                mods[:, 3, n // 2:n // 2 + 1], ALU.mult, ALU.add).then_inc(h2_dve, 1)

            def bcast(s):
                return s.unsqueeze(2).broadcast_to([P, 8, E])

            def centre(g):
                lg = logit[:, g % 2]
                dve.wait_ge(logit_mm, g + 1)
                dve.wait_ge(ld_ffn, 64)
                v.tensor_tensor(lg, bank[g][:, :].rearrange("p (j e) -> p j e", e=E),
                                br_sb[:, :].unsqueeze(1).broadcast_to([P, 8, E]), ALU.add).then_inc(logit_read, 1)
                dve.wait_ge(logit_read, g + 1)
                link(v.tensor_reduce(sm[:, 0, :], lg, AX.X, ALU.max))
                v.tensor_tensor(lg, lg, bcast(sm[:, 0, :]), ALU.subtract).then_inc(centred, 1)

            def normalise(g):
                lg = logit[:, g % 2]
                dve.wait_ge(rexp, g + 1)
                link(v.tensor_reduce(sm[:, 1, :], lg, AX.X, ALU.add))
                link(v.reciprocal(sm[:, 2, :], sm[:, 1, :]))
                v.tensor_tensor(prob[:, 8 * (g % 2):8 * (g % 2) + 8, g // 2, :], lg, bcast(sm[:, 2, :]),
                                ALU.mult).then_inc(prob_ready, 1)

            centre(0)
            for g in range(1, B):
                centre(g)
                normalise(g - 1)
                dve.wait_ge(prob_ready, g)
            normalise(B - 1)
            for g in range(4):
                dve.wait_ge(probt_ready, g + 1)
                link(v.tensor_scalar(keys[:, 0, CH * g:CH * (g + 1)], probt[:, CH * g:CH * (g + 1)],
                                     cst_sb[:, C_SGN:C_SGN + 1], None, ALU.mult))
            dve.sem_inc(keys_made, 1)
            cur = 0

            def exchange(src, dst, dist, mirrored):
                s = keys[:, src, :].rearrange("p (m two d) -> p m two d", two=2, d=dist)
                o = keys[:, dst, :].rearrange("p (m two d) -> p m two d", two=2, d=dist)
                lo, hi = s[:, :, 0, :], s[:, :, 1, :]
                ohi = o[:, :, 1, :]
                if mirrored:
                    hi, ohi = hi[:, :, ::-1], ohi[:, :, ::-1]
                v.tensor_tensor(o[:, :, 0, :], lo, hi, ALU.max)
                link(v.tensor_tensor(ohi, lo, hi, ALU.min))

            dist = 1
            while dist < HT:
                exchange(cur, 1 - cur, dist, True)
                cur = 1 - cur
                d = dist // 2
                while d >= 1:
                    exchange(cur, 1 - cur, d, False)
                    cur = 1 - cur
                    d //= 2
                dist *= 2
            dve.wait_ge(h2_lo, NCH)
            v.tensor_copy(swapped[0:E, :], keys[E:P, cur, :])
            link(v.tensor_copy(swapped[E:P, :], keys[0:E, cur, :]))
            link(v.scalar_tensor_tensor(out=keys[:, 1 - cur, :], in0=swapped[:, :], scalar=-1.0,
                                        in1=keys[:, cur, :], op0=ALU.mult, op1=ALU.max))
            cur = 1 - cur
            d = HT // 2
            while d >= G:
                exchange(cur, 1 - cur, d, False)
                cur = 1 - cur
                d //= 2
            link(v.tensor_scalar(swapped[:, :], keys[:, cur, :], cst_sb[:, C_SGN:C_SGN + 1], None, ALU.mult))
            gv = swapped[:, :].rearrange("p (q g) -> p q g", g=G)
            v.tensor_reduce(gsum[:, :], gv, AX.X, ALU.add)
            v.tensor_reduce(gmin[:, :], gv, AX.X, ALU.min)
            link(v.memset(tau[:, :], 0.0))
            dve.sem_inc(groups_summed, 1)
            base = steps[0]
            with dve.Fori(0, len(SHIFTS)) as r:
                ti = tau[:, :].bitcast(I32).broadcast_to([P, RATIO])
                v.tensor_tensor(cand[:, :].bitcast(I32), ti, bits_sb[:, bass.ds(r * RATIO, RATIO)],
                                ALU.bitwise_or).then_inc(dve_chain, 1)
                dve.wait_ge(dve_chain, r * 4 + (base + 1))
                v.tensor_tensor(cmp[:, :, :], gsum[:, :].unsqueeze(1).broadcast_to([P, RATIO, NG]),
                                cand[:, :].unsqueeze(2).broadcast_to([P, RATIO, NG]),
                                ALU.is_ge).then_inc(dve_chain, 1)
                dve.wait_ge(dve_chain, r * 4 + (base + 2))
                v.tensor_reduce(cnt[:, :], cmp[:, :, :], AX.X, ALU.add).then_inc(cmp_done, 1)
                dve.wait_ge(cnt_mm, r + 1)
                v.scalar_tensor_tensor(out=hit[:, :], in0=bank[7][:, 0:RATIO], scalar=float(GROUPS),
                                       in1=cand[:, :], op0=ALU.is_ge, op1=ALU.mult).then_inc(dve_chain, 1)
                dve.wait_ge(dve_chain, r * 4 + (base + 3))
                v.tensor_reduce(tau[:, :], hit[:, :], AX.X, ALU.max).then_inc(dve_chain, 1)
                dve.wait_ge(dve_chain, r * 4 + (base + 4))
            steps[0] = base + 4 * len(SHIFTS)
            link(v.tensor_scalar(gpen[:, :], gsum[:, :], tau[:, 0:1], NEVER, ALU.is_lt, ALU.mult))
            link(v.tensor_tensor(gpen[:, :], gpen[:, :], gmin[:, :], ALU.max))
            link(v.tensor_reduce(vth[:, 0:1], gpen[:, :], AX.X, ALU.min))
            v.tensor_copy(vth[0:E, 1:2], vth[E:P, 0:1])
            link(v.tensor_copy(vth[E:P, 1:2], vth[0:E, 0:1]))
            link(v.tensor_tensor(vth[:, 2:3], vth[:, 0:1], vth[:, 1:2], ALU.min))
            xt = x_sb[:, :, :, :].rearrange("p b a d -> p (b a) d")
            dve.wait_ge(scores_dup, 64)

            def keep(c):
                g = gated[:, CH * c:CH * (c + 1)]
                v.scalar_tensor_tensor(out=g, in0=g, scalar=vth[:, 2:3], in1=g,
                                       op0=ALU.is_ge, op1=ALU.mult).then_inc(kept_ready, 1)

            def results(n):
                for s, (c, turned, ready, stored) in enumerate(((n + PAIRS, turned_f, res_f, stored_f),
                                                                (n, turned_s, res_s, stored_s))):
                    dve.wait_ge(turned, n + 2)
                    dve.wait_ge(stored, (n + 1) * 16)
                    for j in range(TPC):
                        t = bass.ds(c * TPC + j, 1)
                        v.scalar_tensor_tensor(out=res[:, 1 - s, j, :], in0=bank[6 + s][:, P * j:P * (j + 1)],
                                               scalar=rden[:, j, bass.ds(c, 1)],
                                               in1=xt[:, t, :].rearrange("p o d -> p (o d)"),
                                               op0=ALU.mult, op1=ALU.add).then_inc(ready, 1)

            def lower(n, k):
                dve.wait_ge(hi_ready, n * KT + (k + 1))
                dve.wait_ge(down_f, n * KT + (k + 1))
                v.tensor_tensor(hid_lo[:, k % RING], hid_f[:, k % 2], hid_hi[:, k % RING].bitcast(F32),
                                ALU.subtract).then_inc(lo_dve, 1)

            def hidden(n, first):
                for k in range(KT):
                    dve.wait_ge(gate_mm, n * KT + (k + 1))
                    dve.wait_ge(silu_ready, n * KT + (k + 1))
                    if not (first and k == 0):
                        dve.wait_ge(hid_f_ready, n * KT + k)
                    v.scalar_tensor_tensor(out=glin_f[:, :], in0=bank[2 + k % 2][:, :],
                                           scalar=cols_sb[:, V_GATE + k:V_GATE + k + 1], in1=silu[:, k % 2, :],
                                           op0=ALU.add, op1=ALU.mult).then_inc(gate_used, 1)
                    dve.wait_ge(fetched[k % RING], n * (16 * KT // RING) + 16 * (k // RING + 1))
                    if not (first and k == 0):
                        dve.wait_ge(hid_s_ready, n * KT + k)
                    v.tensor_tensor(glin_s[:, :], back[:, k % RING, 0], back[:, k % RING, 1],
                                    ALU.mult).then_inc(fetch_used, 1)
                    dve.wait_ge(gate_used, n * KT + (k + 1))
                    if k % 2 == 1 and not (first and k < 2):
                        dve.wait_ge(lo_pool, n * (KT // 2) + k // 2)
                    v.tensor_tensor(hid_f[:, k % 2], glin_f[:, :], gated[:, bass.ds(n * CH + HT, CH)],
                                    ALU.mult).then_inc(hid_f_ready, 1)
                    dve.wait_ge(fetch_used, n * KT + (k + 1 + RING))
                    if not (first and k < RING):
                        dve.wait_ge(down_s, n * KT + (k + 1 - RING))
                    v.tensor_tensor(hid_s[:, k % RING], glin_s[:, :], gated[:, bass.ds(n * CH, CH)],
                                    ALU.mult).then_inc(hid_s_ready, 1)
                    if k % 2 == 0:
                        lower(n, k)
                    if first and k < PAIRS - 1:
                        keep(k + 1)
                        keep(k + 1 + PAIRS)
                    if first and k == 8:
                        dve.wait_ge(den_rows, 1)
                        v.tensor_copy(den_sb[:, :], bank[7][0:NCH, :]).then_inc(den_kept, 1)
                    if first and k == 12:
                        dve.wait_ge(den_turned, 1)
                        link(v.tensor_scalar(rden[:, :, :], bank[7][:, 0:TPC * NCH].rearrange(
                            "p (j n) -> p j n", n=NCH), 1e-6, None, ALU.add))
                        link(v.reciprocal(rden[:, :, :], rden[:, :, :]))
                    if k == KT // 2 and not first:
                        results(n - 1)

            keep(PAIRS)
            keep(0)
            dve.wait_ge(kept_ready, 2)
            hidden(0, True)
            dve.wait_ge(kept_ready, NCH)
            with dve.Fori(1, PAIRS) as n:
                hidden(n, False)
            results(PAIRS - 1)

        @block.tensor
        def _(pe):
            mm = nc.tensor.matmul

            pe.wait_ge(ld_mod, 16)
            pe.wait_ge(sc_done, 1)
            for m in range(6):
                mm(bank[0][:, B * m:B * (m + 1)], wmod_sb[:, D * m:D * (m + 1)], sc[:, :], start=True, stop=True)
            pe.wait_ge(scb_done, 1)
            for b in range(B):
                last = mm(bank[1][:, D * b:D * (b + 1)], scb[:, b, :], wmod_sb[:, 2 * D:3 * D],
                          start=True, stop=True)
            last.then_inc(mod_mm, 1)

            pe.wait_ge(ld_tabf, 16)
            pe.wait_ge(mod_read, 1)
            for a in range(AH):
                pe.wait_ge(plus_ready, a + 1)
                pe.wait_ge(minus_ready, a + 1)
                for b in range(B):
                    for par in range(2):
                        last = mm(bank[2 * b + par][:, :], fold[:, par, a, D * b:D * (b + 1)],
                                  tabf_sb[:, a, par, :], start=(a == 0), stop=(a == AH - 1))
                        if a == AH - 1:
                            last.then_inc(fwd_ready, 1)

            def project(i):
                b, par = i // 2, i % 2
                n = NRE[par]
                pe.wait_ge(xf_fixed, b + 1)
                pe.wait_ge(xf_dve, b + 1)
                for s, (done, bk, width, w) in enumerate(((q_mm, bank[par], HALF, W_Q), (k_mm, bank[2], n, W_K),
                                                          (v_mm, bank[3], n, W_V))):
                    if i == 0 and s == 1:
                        pe.wait_ge(xf_act, 2)
                    if i == 0 and s == 2:
                        pe.wait_ge(xf_dve, 2)
                    if s == 0 and i >= 2:
                        pe.wait_ge(sq_ready, i - 1)
                    if s == 1 and i >= 1:
                        pe.wait_ge(prod_ready, i)
                    if s == 2 and i >= 1:
                        pe.wait_ge(v_kept, i)
                    last = mm(bk[:, 0:width], wqkv_sb[:, s, :], xf[:, b, par, 0:width],
                              start=True, stop=(par == 1), skip_group_check=True)
                    if par == 0:
                        last = mm(bk[:, 0:1], rows_sb[0:1, w:w + D], rows_sb[0:1, W_L:W_L + 1],
                                  start=False, stop=True, skip_group_check=True)
                    last.then_inc(done, 1)

            def sum_heads(i):
                b, par = i // 2, i % 2
                n = NRE[par]
                sel = cst_sb[:, C_SEL + BH * b:C_SEL + BH * (b + 1)]
                if i == 0:
                    pe.wait_ge(xf_act, B)
                    pe.wait_ge(xf_dve, B)
                pe.wait_ge(mag_ready, i + 1)
                mm(bank[4 + par][0:BH, 0:n], sel, mag[:, par, 0:n], start=(b == 0), stop=(b == B - 1))
                pe.wait_ge(prod_ready, i + 1)
                mm(bank[6 + par][0:BH, 0:n], sel, prodqk[:, par, 0:n], start=(b == 0),
                   stop=(b == B - 1)).then_inc(head_sums, 1)

            pe.wait_ge(ld_w, 32)
            for i in range(2 * B):
                project(i)
                if i >= 1:
                    sum_heads(i - 1)
            sum_heads(2 * B - 1)

            pe.wait_ge(nsel_ready, 1)
            pe.wait_ge(attn_ready, 1)
            for i in range(2 * B):
                par, b = i // B, i % B
                n, lo = NRE[par], par * NRE[0]
                if i >= 2:
                    pe.wait_ge(ore_ready, i - 1)
                    pe.wait_ge(oim_ready, i - 1)
                exp = cst_sb[0:BH, C_EXP + P * b:C_EXP + P * (b + 1)]
                mm(bank[b % 2][:, 0:n], exp, attn[:, lo:lo + n], start=True, stop=True)
                mm(bank[2 + b % 2][:, 0:n], exp, nsel[:, lo:lo + n], start=True, stop=True).then_inc(spread, 1)

            for i in range(A):
                par = i // AH
                pe.wait_ge(ore_ready, B * (par + 1))
                pe.wait_ge(oim_ready, B * (par + 1))
                if i >= 4:
                    pe.wait_ge(y_act, i - 3)
                for b in range(B):
                    last = mm(bank[4 + i % 4][:, D * b:D * (b + 1)], of[:, b, par, P * (i % AH):P * (i % AH + 1)],
                              wob[:, b, :], start=True, stop=True)
                last.then_inc(y_mm, 1)

            pe.wait_ge(ld_tabi, 16)
            pe.wait_ge(y_fixed, 1)
            for a in range(AH):
                if a >= 2:
                    pe.wait_ge(inv_read, a - 1)
                for par, done in enumerate((inv_even, inv_odd)):
                    for i in range(AH * par, AH * (par + 1)):
                        pe.wait_ge(y_act, i + 1)
                        last = mm(bank[2 * par + a % 2][:, :], tabi_sb[:, i, P * a:P * (a + 1)], yf[:, i, :],
                                  start=(i == AH * par), stop=(i == AH * (par + 1) - 1))
                    last.then_inc(done, 1)

            def turn_in(n):
                if n >= 4:
                    pe.wait_ge(h2_act if n % 2 == 0 else h2_dve, (n - 4) // 2 + 1)
                for j in range(TPC):
                    last = nc.tensor.transpose(bank[4 + n % 4][:, P * j:P * (j + 1)],
                                               xn[:, (n % 2) * TPC + j, n // 2, :], ident)
                last.then_inc(tr_mm, 1)

            def logits(n):
                pe.wait_ge(h2_act if n % 2 == 0 else h2_dve, n // 2 + 1)
                for j in range(TPC):
                    c = ((n % 2) * TPC + j) * E
                    last = mm(bank[n // 2][:, c:c + E], h2t[:, CH * n + P * j:CH * n + P * (j + 1)], wr_sb[:, :],
                              start=True, stop=True)
                if n % 2 == 1:
                    last.then_inc(logit_mm, 1)

            pe.wait_ge(xn_ready, A)
            pe.wait_ge(inv_read, AH)
            pe.wait_ge(ld_ffn, 64)
            for n in range(NCH):
                turn_in(n)
                if n >= 2:
                    logits(n - 2)
            logits(NCH - 2)
            logits(NCH - 1)
            pe.wait_ge(prob_ready, B)
            for g in range(4):
                for j in range(4):
                    last = nc.tensor.transpose(bank[4 + g][:, P * j:P * (j + 1)],
                                               prob[:, 4 * g + j, :, :].rearrange("p h e -> p (h e)"), ident)
                last.then_inc(prob_tr, 1)

            def product3(out_, w_hi, w_lo, m_hi, m_lo, start, stop):
                mm(out_, w_hi, m_hi, start=start, stop=False)
                mm(out_, w_lo, m_hi, start=False, stop=False)
                return mm(out_, w_hi, m_lo, start=False, stop=stop)

            pe.wait_ge(raw_lo, 2)
            pe.wait_ge(h2_lo, NCH)
            with pe.Fori(0, PAIRS) as n:
                hi, lo = h2hi[:, bass.ds(n * CH, CH)], h2lo[:, bass.ds(n * CH, CH)]
                for k in range(KT):
                    pe.wait_ge(silu_held, n * KT + (k + 1))
                    product3(bank[k % 2][:, :], wup_hi[:, k], wup_lo[:, k], hi, lo, True, True).then_inc(pre_up, 1)
                    pe.wait_ge(gate_held, n * KT + (k + 1))
                    product3(bank[2 + k % 2][:, :], wgate_hi[:, k], wgate_lo[:, k], hi, lo, True,
                             True).then_inc(pre_gate, 1)

            pe.wait_ge(probt_ready, 4)
            with pe.Fori(0, len(SHIFTS)) as r:
                pe.wait_ge(cmp_done, r + 1)
                mm(bank[7][:, 0:RATIO], ones, cnt[:, :], start=True, stop=True).then_inc(cnt_mm, 1)

            def up_gate(n, k, fresh=False):
                hi, lo = h2hi[:, bass.ds(n * CH + HT, CH)], h2lo[:, bass.ds(n * CH + HT, CH)]
                if not fresh:
                    pe.wait_ge(silu_ready, n * KT + (k - 1))
                product3(bank[k % 2][:, :], wup_hi[:, k], wup_lo[:, k], hi, lo, True, True).then_inc(up_mm, 1)
                if not fresh:
                    pe.wait_ge(gate_used, n * KT + (k - 1))
                product3(bank[2 + k % 2][:, :], wgate_hi[:, k], wgate_lo[:, k], hi, lo, True,
                         True).then_inc(gate_mm, 1)

            def turn_back(n):
                for s, (ready, read, turned) in enumerate(((out_f, res_f, turned_f), (out_s, res_s, turned_s))):
                    pe.wait_ge(ready, n + 1)
                    pe.wait_ge(read, (n + 1) * TPC)
                    for j in range(TPC):
                        last = nc.tensor.transpose(bank[6 + s][:, P * j:P * (j + 1)],
                                                   outt[:, s, P * j:P * (j + 1)], ident)
                    last.then_inc(turned, 1)

            def begin(n, first):
                if not first:
                    pe.wait_ge(out_f, n)
                    pe.wait_ge(out_s, n)
                mm(bank[4][:, :], bdown_sb[:, :], gated[0:E, bass.ds(n * CH + HT, CH)], start=True, stop=False)
                mm(bank[5][:, :], bdown_sb[:, :], gated[0:E, bass.ds(n * CH, CH)], start=True, stop=False)

            def down(n, k):
                pe.wait_ge(hi_ready, n * KT + (k + 1))
                pe.wait_ge(lo_dve if k % 2 == 0 else lo_pool, n * (KT // 2) + (k // 2 + 1))
                product3(bank[4][:, :], wdown_hi[:, k], wdown_lo[:, k], hid_hi[:, k % RING], hid_lo[:, k % RING],
                         False, k == KT - 1).then_inc(down_f, 1)
                pe.wait_ge(hid_s_ready, n * KT + (k + 1))
                mm(bank[5][:, :], wdown_sb[:, k], hid_s[:, k % RING], start=False,
                   stop=(k == KT - 1)).then_inc(down_s, 1)

            def serve(n, first, final):
                for k in range(KT):
                    if k < KT - 2:
                        up_gate(n, k + 2)
                    elif not final:
                        up_gate(n + 1, k + 2 - KT)
                    if k == 0 and not first:
                        down(n - 1, KT - 1)
                    if k == 1:
                        begin(n, first)
                    if k >= 1:
                        down(n, k - 1)
                    if k == 5 and not first:
                        turn_back(n - 1)
                    if first and k == 5:
                        pe.wait_ge(kept_ready, NCH)
                        for c in range(NCH):
                            last = mm(bank[7][0:NCH, :], cst_sb[0:E, C_ROW + NCH * c:C_ROW + NCH * (c + 1)],
                                      gated[0:E, CH * c:CH * (c + 1)], start=(c == 0), stop=(c == NCH - 1))
                        last.then_inc(den_rows, 1)
                    if first and k == 11:
                        pe.wait_ge(den_kept, 1)
                        for j in range(TPC):
                            last = nc.tensor.transpose(bank[7][:, NCH * j:NCH * (j + 1)],
                                                       den_sb[:, P * j:P * (j + 1)], ident[0:NCH, 0:NCH])
                        last.then_inc(den_turned, 1)

            pe.sem_inc(turned_f, 1)
            pe.sem_inc(turned_s, 1)
            pe.sem_inc(down_f, RING)
            pe.wait_ge(silu_held, PAIRS * KT + 2)
            pe.wait_ge(gate_held, PAIRS * KT + 2)
            up_gate(0, 0, True)
            up_gate(0, 1, True)
            pe.wait_ge(kept_ready, 2)
            pe.wait_ge(raw_lo, 3)
            serve(0, True, False)
            with pe.Fori(1, PAIRS - 1) as n:
                serve(n, False, False)
            serve(PAIRS - 1, False, True)
            down(PAIRS - 1, KT - 1)
            turn_back(PAIRS - 1)


def kernel(L0_attn_query, L0_attn_Wq, L0_attn_bq, L0_attn_Wk, L0_attn_bk, L0_attn_Wv, L0_attn_bv, L0_attn_Wo,
           L0_attn_bo, L0_ffn_Wr, L0_ffn_br, L0_ffn_Wup, L0_ffn_bup, L0_ffn_Wgate, L0_ffn_bgate, L0_ffn_Wdown,
           L0_ffn_bdown, L0_c, L0_wmod):
    import concourse.bacc as bacc
    from concourse.bass_utils import run_bass_kernel_spmd

    def arr(v):
        return np.ascontiguousarray(np.asarray(v))

    def unit_tiles(v):
        return arr(v).T.reshape(KT, P).T

    tabf, tabi = transform_tables()
    arrays = {
        "x": arr(L0_attn_query),
        "cst": constants(),
        "bits": round_bits(),
        "cols": arr(np.concatenate([arr(L0_c).T, unit_tiles(L0_ffn_bup), unit_tiles(L0_ffn_bgate)], axis=1)),
        "rows": arr(np.concatenate([arr(L0_attn_bq), arr(L0_attn_bk), arr(L0_attn_bv), arr(L0_attn_bo),
                                    np.full(1, L, np.float32)])[None, :]),
        "wmod": arr(L0_wmod),
        "wqkv": arr(np.concatenate([arr(L0_attn_Wq), arr(L0_attn_Wk), arr(L0_attn_Wv)], axis=1)),
        "wo": arr(L0_attn_Wo),
        "tabf": tabf,
        "tabi": tabi,
        "wr": arr(L0_ffn_Wr),
        "br": arr(L0_ffn_br),
        "wup": arr(arr(L0_ffn_Wup).transpose(1, 2, 0).reshape(D, E * H)),
        "wgate": arr(arr(L0_ffn_Wgate).transpose(1, 2, 0).reshape(D, E * H)),
        "wdown": arr(arr(L0_ffn_Wdown).transpose(1, 0, 2).reshape(KT, P, D).transpose(1, 0, 2).reshape(P, KT * D)),
        "bdown": arr(L0_ffn_bdown),
    }
    nc = bacc.Bacc("TRN2", target_bir_lowering=False, num_devices=1)
    args = [nc.dram_tensor(f"in_{k}", a.shape, mybir.dt.from_np(a.dtype), kind="ExternalInput").ap()
            for k, a in arrays.items()]
    out = nc.dram_tensor("out_y", (B, L, D), F32, kind="ExternalOutput").ap()
    build(nc, *args, out)
    r = run_bass_kernel_spmd(nc, [{f"in_{k}": a for k, a in arrays.items()}], core_ids=[0])
    return r.results[0]["out_y"]
```

```python
from contextlib import ExitStack

import numpy as np

import concourse.bass as bass
from concourse import mybir

ALU = mybir.AluOpType
ACT = mybir.ActivationFunctionType
F32 = mybir.dt.float32
F32R = mybir.dt.float32r
I32 = mybir.dt.int32
AX = mybir.AxisListType

P = 128
B, L, D = 4, 1024, 128
HEADS, DH = 16, 8
KTOP = 64
A = L // P
AH = A // 2
HALF = L // 2
NF = L // 2 + 1
NRE = (HALF // 2 + 1, HALF // 2)
BH = B * HEADS
E, H, G, KSEL = 64, 32, 64, 16
TOK = B * L
KT = E * H // P
CH = 512
NCH = TOK // CH
TPC = CH // P
RING = 4
BACK = 8
HT = TOK // 2
NG = HT // G
GROUPS = TOK // G * KSEL
HALF_STEPS = (HT // G).bit_length() - 1
EPS = 1e-5
RATIO = 16
SHIFTS = (27, 23, 19, 15, 11, 7, 3, 0)
NEVER = 1e30
assert BACK == KT // 2

C_ID, C_ONE, C_SGN, C_ROW = 0, P, 2 * P, 2 * P + 1
C_ALL = C_ROW + NCH * NCH
S_SEL, S_EXP, S_ALL = 0, B * BH, B * BH + B * P
V_C, V_UP, V_GATE, V_ALL = 0, B, B + KT, B + 2 * KT
W_Q, W_K, W_V, W_O, W_L, W_ALL = 0, P, 2 * P, 3 * P, 4 * P, 4 * P + 1


def transform_tables():
    t = np.arange(HALF)[:, None]
    fwd, inv = [], []
    for par in range(2):
        fre = 2 * np.arange(NRE[par])[None, :] + par
        fim = fre[:, 1:HALF // 2] if par == 0 else fre
        are, aim = 2 * np.pi * ((t * fre) % L) / L, 2 * np.pi * ((t * fim) % L) / L
        fwd.append(np.concatenate([np.cos(are), -np.sin(aim)], axis=1))
        weight = np.where((fre == 0) | (fre == HALF), 1.0, 2.0)
        inv.append(np.concatenate([weight * np.cos(are), -2.0 * np.sin(aim)], axis=1).T / L)
    fwd = np.stack(fwd, axis=1).reshape(AH, P, 2, HALF).transpose(1, 0, 2, 3)
    inv = np.concatenate(inv, axis=0).reshape(A, P, HALF).transpose(1, 0, 2)
    return (np.ascontiguousarray(fwd.reshape(P, -1), dtype=np.float32),
            np.ascontiguousarray(inv.reshape(P, -1), dtype=np.float32))


def constants():
    c = np.zeros((P, C_ALL), np.float32)
    c[:, C_ID:C_ID + P] = np.eye(P)
    c[:, C_ONE:C_ONE + P] = 1.0
    c[:, C_SGN] = np.where(np.arange(P) < E, 1.0, -1.0)
    for n in range(NCH):
        c[:, C_ROW + n * NCH + n] = 1.0
    return c


def selectors():
    c = np.zeros((P, S_ALL), np.float32)
    for b in range(B):
        for ch in range(D):
            row = b * HEADS + ch // DH
            c[ch, S_SEL + b * BH + row] = 1.0
            c[row, S_EXP + b * P + ch] = 1.0
    return c


def round_bits():
    bits = np.zeros((len(SHIFTS), RATIO), np.int32)
    for r, s in enumerate(SHIFTS):
        width = (SHIFTS[r - 1] if r else 31) - s
        bits[r] = np.minimum(np.arange(RATIO), 2 ** width - 1).astype(np.int32) << s
    return np.ascontiguousarray(np.broadcast_to(bits.reshape(1, -1), (P, bits.size)))


def sort_plan():
    plan, left, m = [], (NCH - 1) * KT // 2, 1
    while m < HT:
        d = m
        while d >= 1:
            pairs = 0 if len(plan) < 3 else min(left, 1)
            plan.append((m, d, pairs))
            left -= pairs
            d //= 2
        m *= 2
    assert left == 0
    return plan


def build(nc, x, cst, sel, bits, cols, rows, wmod, wqkv, wo, tabf, tabi, wr, br, wup, wgate, wdown, bdown, out):
    with ExitStack() as ctx:
        def sem(name):
            return ctx.enter_context(nc.semaphore(name))

        bank = [ctx.enter_context(nc.psum_tensor(f"bank{i}", [P, 512], F32)) for i in range(8)]

        size = 4 * TOK
        top = [-(-nc.sbuf_base // 32) * 32]

        def region(nbytes):
            at = top[0]
            top[0] += -(-nbytes // 32) * 32
            return [at, at + nbytes]

        def put(reg, name, shape, dt=F32):
            at = reg[0]
            reg[0] += -(-int(np.prod(shape[1:])) * 4 // 32) * 32
            assert reg[0] <= reg[1], name
            return nc.alloc_sbuf_tensor_at(name, shape, dt, offset=at)

        def stage(reg):
            return list(reg)

        def sb(name, shape, dt=F32):
            return put(region(-(-int(np.prod(shape[1:])) * 4 // 32) * 32), name, shape, dt)

        r_xn, r_fold, r_table, r_tabi, r_freq, r_q, r_of, r_yf = (region(size) for _ in range(8))
        r_tabi_freq = [r_tabi[0], r_freq[1]]
        r_vf = region(-(-4 * B * NF // 32) * 32)
        r_att = region(4 * (KT * D + 2 * 2 * CH))

        x_sb = sb("x_sb", [P, B, A, D])
        xn = put(stage(r_xn), "xn", [P, A, B, D])
        fold = put(stage(r_fold), "fold", [P, 2, AH, B * D])
        tabf_sb = put(stage(r_table), "tabf_sb", [P, AH, 2, HALF])
        tabi_sb = put(stage(r_tabi), "tabi_sb", [P, A, HALF])
        xf = put(stage(r_freq), "xf", [P, B, 2, HALF])
        qf = put(stage(r_q), "qf", [P, B, 2, HALF])
        vf = put(stage(r_vf), "vf", [P, B, NF])
        s = stage(r_of)
        w_raw = [put(s, f"w_raw{i}", [P, KT, P]) for i in range(2)]
        of = put(stage(r_of), "of", [P, B, 2, HALF])
        s = stage(r_yf)
        sq = put(s, "sq", [P, 2, HALF])
        e2 = put(s, "e2", [P, 2, NRE[0]])
        mag = put(s, "mag", [P, 2, NRE[0]])
        prodqk = put(s, "prodqk", [P, 2, NRE[0]])
        s = stage(r_yf)
        scb = put(s, "scb", [P, B, P])
        gsign = put(s, "gsign", [P, B * D])
        gabs = put(s, "gabs", [P, B * D])
        yf = put(stage(r_yf), "yf", [P, A, B * D])
        s = stage(r_fold)
        energy = put(s, "energy", [BH, NF])
        nsel = put(s, "nsel", [BH, NF + 1], F32R)
        masked = put(s, "masked", [BH, NF])
        sel_sb = put(s, "sel_sb", [P, S_ALL])
        exp_sel = put(s, "exp_sel", [BH, B * P], F32R)
        attn = put(s, "attn", [BH, NF])
        av = put(s, "av", [P, NRE[0]])
        s = stage(r_att)
        wmod_sb = put(s, "wmod_sb", [P, 6 * D])
        wqkv_sb = put(s, "wqkv_sb", [P, 3, D])
        wo_sb = put(s, "wo_sb", [P, D])
        gval = put(s, "gval", [P, B * D])
        wob = put(s, "wob", [P, B, D])
        bol = put(s, "bol", [1, B * D])
        tsum = put(stage(r_q), "tsum", [P, 2, B * D])
        h2t = put(stage(r_fold), "h2t", [P, TOK])
        h2hi = put(stage(r_of), "h2hi", [P, TOK], F32R)
        h2lo = put(stage(r_yf), "h2lo", [P, TOK], F32R)
        logit = put(stage(r_vf), "logit", [P, 2, 8, E])
        s = stage(r_freq)
        prob = put(s, "prob", [P, HT // P, 2, E])
        probt = put(s, "probt", [P, HT])
        keys = put(stage(r_table), "keys", [P, 2, HT])
        gated = put(stage(r_q), "gated", [P, TOK])
        s = stage(r_fold)
        swapped = put(s, "swapped", [P, HT])
        cmp = put(s, "cmp", [P, RATIO, NG])
        kept_hi = put(stage(r_of), "kept_hi", [E, TOK], F32R)
        kept_lo = put(stage(r_yf), "kept_lo", [E, TOK], F32R)
        silu = put(stage(r_vf), "silu", [P, 2, 2, CH])
        held = put(stage(r_xn), "held", [P, RING, 2, CH])
        back = put(stage(r_tabi_freq), "back", [P, BACK, 2, CH])
        s = stage(r_table)
        hid = put(s, "hid", [P, RING, CH])
        outt = put(s, "outt", [P, 2, CH])
        s = stage(r_fold)
        s[0] += 4 * HT
        res = put(s, "res", [P, 2, TPC, D])
        den_sb = put(s, "den_sb", [NCH, CH])
        bdown_hi = put(s, "bdown_hi", [E, D], F32R)
        bdown_lo = put(s, "bdown_lo", [E, D], F32R)
        row_sel = put(s, "row_sel", [E, NCH * NCH], F32R)

        cst_sb = sb("cst_sb", [P, C_ALL])
        bits_sb = sb("bits_sb", [P, len(SHIFTS) * RATIO], I32)
        cols_sb = sb("cols_sb", [P, V_ALL])
        rows_sb = sb("rows_sb", [1, W_ALL])
        wr_sb = sb("wr_sb", [P, E])
        br_sb = sb("br_sb", [1, E])
        wup_hi = sb("wup_hi", [P, KT, P], F32R)
        wup_lo = sb("wup_lo", [P, KT, P], F32R)
        wgate_hi = sb("wgate_hi", [P, KT, P], F32R)
        wgate_lo = sb("wgate_lo", [P, KT, P], F32R)
        s = stage(r_att)
        wdown_sb = put(s, "wdown_sb", [P, KT, D])
        gate = put(s, "gate", [P, 2, 2, CH])
        bdown_sb = sb("bdown_sb", [E, D])
        sc = sb("sc", [P, B])
        mods = sb("mods", [P, 6, B])
        camod = sb("camod", [P, 2, B])
        sal = sb("sal", [P, B])
        gb8 = sb("gb8", [P, B, 2])
        stats = sb("stats", [P, B, A, 6])
        lns = sb("lns", [P, 8, B, 2])
        acc = sb("acc", [P, 2, B, 2])
        qmean = sb("qmean", [P, 2, B])
        top8 = sb("top8", [BH, 8])
        hstat = sb("hstat", [BH, 4])
        sm = sb("sm", [P, 2, 4, 8])
        gsum = sb("gsum", [P, NG])
        gmin = sb("gmin", [P, NG])
        cand = sb("cand", [P, RATIO])
        cnt = sb("cnt", [P, RATIO])
        hit = sb("hit", [P, RATIO])
        tau = sb("tau", [P, 1])
        gpen = sb("gpen", [P, NG])
        vth = sb("vth", [P, 3])
        rden = sb("rden", [P, TPC, NCH])
        assert top[0] <= nc.sbuf_usable_end, (top[0], nc.sbuf_usable_end)

        ident = cst_sb[:, C_ID:C_ID + P]
        ones = cst_sb[:, C_ONE:C_ONE + P]
        gb_chunk = gb8[:, :, :].rearrange("p b c -> p (b c)")

        ld_c = sem("ld_c")
        ld_x = [sem(f"ld_x{a}") for a in range(AH)]
        ld_mod = sem("ld_mod")
        ld_tabf = [sem(f"ld_tabf{a}") for a in range(AH)]
        ld_cst = sem("ld_cst")
        ld_sel = sem("ld_sel")
        ld_w = sem("ld_w")
        ld_tabi = sem("ld_tabi")
        ld_ffn = sem("ld_ffn")
        ld_down = sem("ld_down")
        sc_done = sem("sc_done")
        scb_done = sem("scb_done")
        mod_mm = sem("mod_mm")
        mod_read = sem("mod_read")
        var_ready = sem("var_ready")
        std_ready = sem("std_ready")
        xn_ready = sem("xn_ready")
        xn_act = sem("xn_act")
        plus_ready = sem("plus_ready")
        minus_ready = sem("minus_ready")
        fwd_ready = sem("fwd_ready")
        xf_act = sem("xf_act")
        xf_dve = sem("xf_dve")
        xf_fixed = sem("xf_fixed")
        q_mm = sem("q_mm")
        k_mm = sem("k_mm")
        v_mm = sem("v_mm")
        q_kept = sem("q_kept")
        sq_ready = sem("sq_ready")
        e2_ready = sem("e2_ready")
        mag_ready = sem("mag_ready")
        prod_ready = sem("prod_ready")
        v_kept = sem("v_kept")
        head_sums = sem("head_sums")
        en_read = sem("en_read")
        smax_ready = sem("smax_ready")
        exp_ready = sem("exp_ready")
        attn_ready = sem("attn_ready")
        nsel_ready = sem("nsel_ready")
        sel_ready = sem("sel_ready")
        qmean_ready = sem("qmean_ready")
        spread = sem("spread")
        oim_ready = sem("oim_ready")
        ore_ready = sem("ore_ready")
        y_mm = sem("y_mm")
        y_act = sem("y_act")
        y_fixed = sem("y_fixed")
        inv_even = sem("inv_even")
        inv_odd = sem("inv_odd")
        inv_read = sem("inv_read")
        tr_mm = sem("tr_mm")
        shift_ready = sem("shift_ready")
        h2_act = sem("h2_act")
        h2_dve = sem("h2_dve")
        logit_mm = sem("logit_mm")
        max_ready = sem("max_ready")
        rexp = sem("rexp")
        prob_ready = sem("prob_ready")
        prob_tr = sem("prob_tr")
        probt_ready = sem("probt_ready")
        sort_step = sem("sort_step")
        sort_copy = sem("sort_copy")
        rows_sorted = sem("rows_sorted")
        rows_copied = sem("rows_copied")
        groups_sorted = sem("groups_sorted")
        signs_back = sem("signs_back")
        cmp_done = sem("cmp_done")
        cnt_mm = sem("cnt_mm")
        dve_chain = sem("dve_chain")
        raw_loaded = [sem(f"raw_loaded{i}") for i in range(3)]
        raw_hi = sem("raw_hi")
        raw_lo = sem("raw_lo")
        h2_hi = sem("h2_hi")
        h2_lo = sem("h2_lo")
        scores_dup = sem("scores_dup")
        keys_made = sem("keys_made")
        up_mm = sem("up_mm")
        gate_mm = sem("gate_mm")
        silu_ready = sem("silu_ready")
        gate_kept = sem("gate_kept")
        pair_made = sem("pair_made")
        put_off = [sem(f"put_off{i}") for i in range(RING)]
        fetched = [sem(f"fetched{i}") for i in range(BACK)]
        kept_ready = sem("kept_ready")
        kept_hi_ready = sem("kept_hi_ready")
        kept_lo_ready = sem("kept_lo_ready")
        hid_ready = sem("hid_ready")
        down_mm = sem("down_mm")
        out_ready = sem("out_ready")
        turned = sem("turned")
        res_ready = sem("res_ready")
        stored = [sem(f"stored{i}") for i in range(2)]
        den_rows = sem("den_rows")
        den_kept = sem("den_kept")
        den_turned = sem("den_turned")

        spill = nc.dram_tensor("spill", [NCH * KT // 2, P, 2, CH], F32, kind="Internal").ap()

        block = ctx.enter_context(nc.Block())

        def pair(view, a):
            return view[:, :, a:a + AH + 1:AH]

        def group(view, g):
            return view.rearrange("p (c a q) -> p c a q", a=AH, q=P)[:, :, g, :]

        def batch(view, g, b):
            return view[:, L * b:L * (b + 1)].rearrange("p (c a q) -> p c a q", a=AH, q=P)[:, :, g, :]

        plan = sort_plan()
        logit_bank = (bank[6], bank[0], bank[2], bank[6])

        @block.sync
        def _(sp):
            xv = x.rearrange("b (a p) d -> a p b d", p=P)
            tabv = tabf.rearrange("p (a s c) -> p a s c", a=AH, s=2)
            for a in range(AH):
                for t in (a, a + AH):
                    sp.dma_start(x_sb[:, :, t, :], xv[t]).then_inc(ld_x[a], 16)
                sp.dma_start(tabf_sb[:, a], tabv[:, a]).then_inc(ld_tabf[a], 16)
            sp.dma_start(cst_sb[:, :], cst).then_inc(ld_cst, 16)
            sp.dma_start(wqkv_sb[:, :, :], wqkv.rearrange("d (s n) -> d s n", s=3)).then_inc(ld_w, 16)
            sp.dma_start(wo_sb[:, :], wo).then_inc(ld_w, 16)
            sp.dma_start(tabi_sb[:, :, :], tabi.rearrange("p (a n) -> p a n", a=A)).then_inc(ld_tabi, 16)
            sp.dma_start(wr_sb[:, :], wr).then_inc(ld_ffn, 16)
            sp.dma_start(br_sb[:, :], br.rearrange("(o e) -> o e", o=1)).then_inc(ld_ffn, 16)
            sp.dma_start(bits_sb[:, :], bits).then_inc(ld_ffn, 16)
            for i, w in enumerate((wup, wgate)):
                sp.dma_start(w_raw[i][:, :, :], w.rearrange("d (k n) -> d k n", k=KT)).then_inc(raw_loaded[i], 16)
            sp.dma_start(bdown_sb[:, :], bdown).then_inc(raw_loaded[2], 16)
            sp.wait_ge(fwd_ready, 2 * B)
            sp.dma_start(sel_sb[:, :], sel).then_inc(ld_sel, 16)
            for i in range(RING):
                sp.sem_inc(put_off[i], 16)
            sp.wait_ge(prob_ready, AH)
            sp.dma_start(wdown_sb[:, :, :], wdown.rearrange("p (k n) -> p k n", k=KT)).then_inc(ld_down, 16)
            sp.wait_ge(probt_ready, 4)
            for half in range(2):
                for unit in range(2):
                    sp.dma_start(gated[E * unit:E * unit + E, HT * half:HT * half + HT],
                                 probt[E * half:E * half + E, :]).then_inc(scores_dup, 16)

            def spill_chunk(n):
                for j in range(KT // 2):
                    sp.wait_ge(pair_made, n * (KT // 2) + (j + 3))
                    sp.dma_start(spill[bass.ds(n * (KT // 2) + j, 1)].rearrange("o p s c -> (o p) s c"),
                                 held[:, j % RING]).then_inc(put_off[j % RING], 16)

            def fetch_chunk(n):
                for j in range(BACK):
                    sp.wait_ge(hid_ready, n * KT + (2 * j + 2))
                    sp.dma_start(back[:, j], spill[bass.ds(n * BACK + j, 1)].rearrange("o p s c -> (o p) s c")
                                 ).then_inc(fetched[j], 16)

            with sp.Fori(0, NCH - 1) as n:
                spill_chunk(n)
            for i in range(RING):
                sp.wait_ge(put_off[i], 16 * ((NCH - 1) * KT // 2 // RING + 1))
            sp.wait_ge(scores_dup, 64)
            sp.wait_ge(keys_made, 1)
            fetch_chunk(0)
            spill_chunk(NCH - 1)
            for i in range(RING):
                sp.wait_ge(put_off[i], 16 * (NCH * KT // 2 // RING + 1))
            with sp.Fori(1, NCH) as n:
                fetch_chunk(n)
            for s in range(2):
                sp.wait_ge(stored[s], 16 * (NCH // 2 + 1))

        @block.gpsimd
        def _(pool):
            for a in range(AH):
                pool.wait_ge(xn_ready, a + 1)
                nc.gpsimd.tensor_tensor(fold[:, 1, a, :].rearrange("p (b d) -> p b d", b=B),
                                        xn[:, a], xn[:, a + AH], ALU.subtract).then_inc(minus_ready, 1)

            def split(i, w, hi, lo):
                pool.wait_ge(raw_loaded[i], 16)
                nc.gpsimd.tensor_copy(hi, w).then_inc(raw_hi, 1)
                pool.wait_ge(raw_hi, i + 1)
                nc.gpsimd.tensor_tensor(lo, w, hi.bitcast(F32), ALU.subtract).then_inc(raw_lo, 1)

            split(0, w_raw[0][:, :, :], wup_hi[:, :, :], wup_lo[:, :, :])
            split(1, w_raw[1][:, :, :], wgate_hi[:, :, :], wgate_lo[:, :, :])
            pool.wait_ge(inv_odd, AH)
            for n in range(NCH):
                pool.wait_ge(h2_hi, n + 1)
                c = slice(CH * n, CH * (n + 1))
                nc.gpsimd.tensor_tensor(h2lo[:, c], h2t[:, c], h2hi[:, c].bitcast(F32),
                                        ALU.subtract).then_inc(h2_lo, 1)
            pool.wait_ge(h2_lo, NCH)
            split(2, bdown_sb[:, :], bdown_hi[:, :], bdown_lo[:, :])
            for n in range(NCH):
                pool.wait_ge(kept_hi_ready, n + 1)
                c = slice(CH * n, CH * (n + 1))
                nc.gpsimd.tensor_tensor(kept_lo[:, c], gated[0:E, c], kept_hi[:, c].bitcast(F32),
                                        ALU.subtract).then_inc(kept_lo_ready, 1)

        @block.scalar
        def _(act):
            act.dma_start(cols_sb[:, :], cols).then_inc(ld_c, 16)
            act.dma_start(rows_sb[:, :], rows).then_inc(ld_c, 16)
            act.dma_start(wmod_sb[:, :], wmod).then_inc(ld_mod, 16)

            def std(n):
                act.wait_ge(var_ready, n + 1)
                nc.scalar.activation(lns[:, 5], lns[:, 4], ACT.Sqrt).then_inc(std_ready, 1)

            for a in range(AH):
                std(a)
                if a == 0:
                    act.wait_ge(ld_c, 32)
                    nc.scalar.activation(sc[:, :], cols_sb[:, V_C:V_C + B], ACT.Silu).then_inc(sc_done, 1)
                    nc.scalar.activation(scb[:, :, :], cols_sb[:, V_C:V_C + B].unsqueeze(2).broadcast_to([P, B, P]),
                                         ACT.Silu).then_inc(scb_done, 1)
            for b in range(B):
                act.wait_ge(fwd_ready, 2 * b + 1)
                act.wait_ge(mod_read, 2)
                nc.scalar.activation(xf[:, b, 0, :], bank[2 * b][:, :], ACT.Copy,
                                     scale=camod[:, 0, b:b + 1]).then_inc(xf_act, 1)

            def magnitude(i):
                act.wait_ge(e2_ready, i + 1)
                if i >= 2:
                    act.wait_ge(head_sums, i - 1)
                par = i % 2
                nc.scalar.activation(mag[:, par, 0:NRE[par]], e2[:, par, 0:NRE[par]],
                                     ACT.Sqrt).then_inc(mag_ready, 1)

            for i in range(2 * B):
                b, par = i // 2, i % 2
                n = NRE[par]
                act.wait_ge(q_mm, i + 1)
                nc.scalar.activation(qf[:, b, par, 0:n], bank[par][:, 0:n], ACT.Copy,
                                     accum_out=acc[:, 0, b, par:par + 1])
                nc.scalar.activation(qf[:, b, par, n:HALF], bank[par][:, n:HALF], ACT.Copy,
                                     accum_out=acc[:, 1, b, par:par + 1]).then_inc(q_kept, 1)
                if i >= 2:
                    act.wait_ge(e2_ready, i - 1)
                nc.scalar.activation(sq[:, par, :], bank[par][:, :], ACT.Square).then_inc(sq_ready, 1)
                if i >= 1:
                    magnitude(i - 1)
            magnitude(2 * B - 1)
            act.wait_ge(ld_sel, 16)
            nc.scalar.copy(exp_sel[:, :], sel_sb[0:BH, S_EXP:S_EXP + B * P]).then_inc(sel_ready, 1)
            act.wait_ge(smax_ready, 1)
            nc.scalar.activation(attn[:, :], masked[:, :], ACT.Exp, bias=hstat[:, 1:2],
                                 scale=1.0 / (DH ** 0.5 + 1e-8), accum_out=hstat[:, 2:3]).then_inc(exp_ready, 1)
            act.wait_ge(qmean_ready, 1)
            act.wait_ge(raw_lo, 2)
            for i in range(2 * B):
                par, b = i // B, i % B
                act.wait_ge(spread, i + 1)
                nc.scalar.activation(of[:, b, par, NRE[par]:HALF], bank[2 + b % 2][:, 1:HALF // 2 + par],
                                     ACT.Copy, scale=qmean[:, 1, b:b + 1]).then_inc(oim_ready, 1)
            for i in range(A):
                act.wait_ge(y_mm, i + 1)
                nc.scalar.copy(yf[:, i, :], bank[4 + i % 4][:, :]).then_inc(y_act, 1)

            def normalise(a):
                if a >= 1:
                    act.wait_ge(xn_act, a)
                    act.wait_ge(xn_ready, AH + a)
                std(AH + a)
                act.wait_ge(shift_ready, a + 1)
                for b in range(2):
                    for s, t in enumerate((a, a + AH)):
                        ins = nc.scalar.activation(xn[:, t, b, :], x_sb[:, b, t, :], ACT.Identity,
                                                   scale=lns[:, 5, b, s:s + 1], bias=lns[:, 7, b, s:s + 1])
                ins.then_inc(xn_act, 1)

            def modulate(g):
                act.wait_ge(tr_mm, g + 1)
                for b in range(2):
                    nc.scalar.activation(batch(h2t, g, b),
                                         bank[4][:, 2 * P * b:2 * P * (b + 1)].rearrange("p (s q) -> p s q", s=2),
                                         ACT.Identity, scale=camod[:, 1, b:b + 1],
                                         bias=mods[:, 3, b:b + 1]).then_inc(h2_act, 1)

            def exponents(g):
                act.wait_ge(max_ready, g + 1)
                if g >= 2:
                    act.wait_ge(prob_ready, g - 1)
                for j in range(8):
                    ins = nc.scalar.activation(logit[:, g % 2, j, :], logit_bank[g][:, E * j:E * (j + 1)], ACT.Exp,
                                               bias=sm[:, g % 2, 1, j:j + 1], accum_out=sm[:, g % 2, 2, j:j + 1])
                ins.then_inc(rexp, 1)

            def keep_probs(g):
                act.wait_ge(prob_tr, g + 1)
                nc.scalar.copy(group(probt[:, :], g), bank[7][:, :].rearrange("p (c q) -> p c q", q=P)
                               ).then_inc(probt_ready, 1)

            normalise(0)
            normalise(1)
            modulate(0)
            normalise(2)
            modulate(1)
            exponents(0)
            normalise(3)
            modulate(2)
            exponents(1)
            modulate(3)
            exponents(2)
            keep_probs(0)
            exponents(3)
            keep_probs(1)
            keep_probs(2)
            keep_probs(3)
            act.wait_ge(h2_act, 2 * AH)
            act.wait_ge(h2_dve, 2 * AH)
            for n in range(NCH):
                nc.scalar.activation(h2hi[:, CH * n:CH * (n + 1)], h2t[:, CH * n:CH * (n + 1)],
                                     ACT.Copy).then_inc(h2_hi, 1)

            act.sem_inc(silu_ready, 2)
            act.sem_inc(gate_kept, RING)

            def factors(q):
                act.wait_ge(pair_made, q + 1)
                for i in (2 * q, 2 * q + 1):
                    k = i % KT
                    act.wait_ge(up_mm, i + 1)
                    nc.scalar.activation(silu[:, q % 2, i % 2], bank[k % 2][:, :], ACT.Silu,
                                         bias=cols_sb[:, V_UP + k:V_UP + k + 1]).then_inc(silu_ready, 1)
                    act.wait_ge(gate_mm, i + 1)
                    nc.scalar.activation(gate[:, q % 2, i % 2], bank[2 + k % RING][:, :], ACT.Identity,
                                         bias=cols_sb[:, V_GATE + k:V_GATE + k + 1]).then_inc(gate_kept, 1)

            pairs = [step[2] for step in plan]
            copies = 0
            for i, (m, d, _pairs) in enumerate(plan):
                if d < m:
                    act.wait_ge(sort_step, i)
                    act.wait_ge(sort_copy, copies)
                    src, dst = (keys[:, b, :].rearrange("p (n q d) -> p n q d", q=2 * m // d, d=d)
                                for b in (i % 2, 1 - i % 2))
                    nc.scalar.copy(dst[:, :, ::2 * m // d - 1, :], src[:, :, ::2 * m // d - 1, :]
                                   ).then_inc(sort_copy, 1)
                    copies += 1
                for q in range(sum(pairs[:i + 1]), sum(pairs[:i + 2])):
                    factors(q)
            act.wait_ge(rows_sorted, 1)
            nc.scalar.copy(swapped[E:P, :], keys[0:E, len(plan) % 2, :]).then_inc(rows_copied, 1)
            act.wait_ge(groups_sorted, 1)
            nc.scalar.activation(swapped[:, :], keys[:, (len(plan) + 1 + HALF_STEPS) % 2, :], ACT.Copy,
                                 scale=cst_sb[:, C_SGN:C_SGN + 1]).then_inc(signs_back, 1)
            for q in range(sum(pairs), NCH * KT // 2):
                factors(q)

            act.wait_ge(h2_lo, NCH)
            act.wait_ge(ld_cst, 16)
            nc.scalar.copy(row_sel[:, :], cst_sb[0:E, C_ROW:C_ALL])
            act.wait_ge(gate_mm, NCH * KT)
            for n in range(NCH):
                act.wait_ge(kept_ready, n + 1)
                nc.scalar.activation(kept_hi[:, CH * n:CH * (n + 1)], gated[0:E, CH * n:CH * (n + 1)],
                                     ACT.Copy).then_inc(kept_hi_ready, 1)

            ov = out.rearrange("b (c j p) d -> (b c) p j d", j=TPC, p=P)
            for s in range(2):
                act.sem_inc(stored[s], 16)
            with act.Fori(0, NCH // 2) as n:
                for s in range(2):
                    act.wait_ge(down_mm, n * (2 * KT) + ((s + 1) * KT + RING))
                    act.wait_ge(turned, n * 2 + (s + 1))
                    nc.scalar.activation(outt[:, s], bank[4 + s][:, :], ACT.Copy,
                                         scale=gb_chunk[:, bass.ds(n * 2 + s, 1)]).then_inc(out_ready, 1)
                    act.wait_ge(res_ready, n * (2 * TPC) + (s + 3) * TPC)
                    act.dma_start(ov[bass.ds(n * 2 + s, 1)].rearrange("o p j d -> (o p) j d"),
                                  res[:, s]).then_inc(stored[s], 16)

        @block.vector
        def _(dve):
            steps = [0]

            def link(ins):
                steps[0] += 1
                ins.then_inc(dve_chain, 1)
                dve.wait_ge(dve_chain, steps[0])

            v = nc.vector
            dve.sem_inc(hid_ready, 2 * BACK)
            dve.sem_inc(res_ready, 2 * TPC)
            dve.sem_inc(pair_made, 2)

            def ln_stats(a):
                for b in range(B):
                    for t in (a, a + AH):
                        ins = v.bn_stats(stats[:, b, t, :], x_sb[:, b, t, :])
                link(ins)
                st = pair(stats, a)
                me, m2e, mo, m2o = st[:, :, :, 1], st[:, :, :, 2], st[:, :, :, 4], st[:, :, :, 5]
                v.tensor_tensor(lns[:, 0], me, mo, ALU.add)
                v.tensor_tensor(lns[:, 1], me, mo, ALU.subtract)
                link(v.tensor_tensor(lns[:, 2], m2e, m2o, ALU.add))
                v.tensor_scalar(lns[:, 6], lns[:, 0], 0.5, None, ALU.mult)
                v.scalar_tensor_tensor(out=lns[:, 3], in0=lns[:, 1], scalar=0.25, in1=lns[:, 1],
                                       op0=ALU.mult, op1=ALU.mult)
                link(v.tensor_scalar(lns[:, 2], lns[:, 2], 1.0 / D, EPS, ALU.mult, ALU.add))
                v.tensor_tensor(lns[:, 4], lns[:, 3], lns[:, 2], ALU.add).then_inc(var_ready, 1)

            def ln_apply(n, a):
                dve.wait_ge(std_ready, n + 1)
                link(v.reciprocal(lns[:, 5], lns[:, 5]))
                for b in range(B):
                    for s, t in enumerate((a, a + AH)):
                        ins = v.tensor_scalar(xn[:, t, b, :], x_sb[:, b, t, :], lns[:, 6, b, s:s + 1],
                                              lns[:, 5, b, s:s + 1], ALU.subtract, ALU.mult)
                ins.then_inc(xn_ready, 1)

            def modulation():
                dve.wait_ge(mod_mm, 1)
                v.tensor_copy(mods[:, :, :], bank[6][:, 0:6 * B].rearrange("p (m b) -> p m b", b=B))
                link(v.tensor_copy(gval[:, :], bank[7][:, :]))
                dve.sem_inc(mod_read, 1)
                v.tensor_scalar(camod[:, 0, :], mods[:, 1, :], 1.0, None, ALU.add)
                v.tensor_scalar(camod[:, 1, :], mods[:, 4, :], 1.0, None, ALU.add)
                v.tensor_scalar(sal[:, :], mods[:, 0, :], float(L), None, ALU.mult)
                link(away_from_zero(gb8[:, :, 0], mods[:, 5, :], B))
                v.tensor_copy(gb8[:, :, 1], gb8[:, :, 0])
                away_from_zero(gval[:, :], gval[:, :], B * D).then_inc(mod_read, 1)

            def away_from_zero(out_, g, n):
                link(v.tensor_scalar(gsign[:, 0:n], g, 0.0, None, ALU.is_ge))
                v.tensor_scalar(gsign[:, 0:n], gsign[:, 0:n], 2.0, -1.0, ALU.mult, ALU.add)
                link(v.scalar_tensor_tensor(out=gabs[:, 0:n], in0=g, scalar=-1.0, in1=g, op0=ALU.mult, op1=ALU.max))
                return v.scalar_tensor_tensor(out=out_, in0=gabs[:, 0:n], scalar=0.25, in1=gsign[:, 0:n],
                                              op0=ALU.max, op1=ALU.mult)

            for a in range(AH):
                dve.wait_ge(ld_x[a], 32)
                ln_stats(a)
                ln_apply(a, a)
                dve.wait_ge(xn_ready, a + 1)
                v.tensor_tensor(fold[:, 0, a, :].rearrange("p (b d) -> p b d", b=B),
                                xn[:, a], xn[:, a + AH], ALU.add).then_inc(plus_ready, 1)
                if a == 1:
                    modulation()
            dve.wait_ge(ld_w, 32)
            dve.wait_ge(mod_read, 2)
            v.tensor_tensor(wob[:, :, :], wo_sb[:, :].unsqueeze(1).broadcast_to([P, B, D]),
                            gval[:, :].rearrange("p (b d) -> p b d", b=B), ALU.mult)
            link(v.scalar_tensor_tensor(out=bol[:, :].rearrange("p (b d) -> p b d", b=B),
                                        in0=rows_sb[0:1, W_O:W_O + D].unsqueeze(1).broadcast_to([1, B, D]),
                                        scalar=float(L), in1=gval[0:1, :].rearrange("p (b d) -> p b d", b=B),
                                        op0=ALU.mult, op1=ALU.mult))
            for b in range(B):
                dve.wait_ge(fwd_ready, 2 * b + 2)
                v.tensor_scalar(xf[:, b, 1, :], bank[2 * b + 1][:, :], camod[:, 0, b:b + 1], None,
                                ALU.mult).then_inc(xf_dve, 1)
                dve.wait_ge(xf_act, b + 1)
                v.tensor_tensor(xf[:, b, 0, 0:1], xf[:, b, 0, 0:1], sal[:, b:b + 1],
                                ALU.add).then_inc(xf_fixed, 1)
            for i in range(2 * B):
                b, par = i // 2, i % 2
                n = NRE[par]
                if i >= 2:
                    dve.wait_ge(head_sums, i - 1)
                dve.wait_ge(k_mm, i + 1)
                dve.wait_ge(q_kept, i + 1)
                v.tensor_tensor(prodqk[:, par, 0:n], bank[2][:, 0:n], qf[:, b, par, 0:n],
                                ALU.mult).then_inc(prod_ready, 1)
                dve.wait_ge(v_mm, i + 1)
                v.tensor_copy(vf[:, b, par * NRE[0]:par * NRE[0] + n], bank[3][:, 0:n]).then_inc(v_kept, 1)
                dve.wait_ge(sq_ready, i + 1)
                if i >= 2:
                    dve.wait_ge(mag_ready, i - 1)
                if par == 0:
                    v.tensor_copy(e2[:, 0, 0:HALF // 2 + 1:HALF // 2], sq[:, 0, 0:HALF // 2 + 1:HALF // 2])
                    v.tensor_tensor(e2[:, 0, 1:HALF // 2], sq[:, 0, 1:HALF // 2], sq[:, 0, n:HALF],
                                    ALU.add).then_inc(e2_ready, 1)
                else:
                    v.tensor_tensor(e2[:, 1, 0:n], sq[:, 1, 0:n], sq[:, 1, n:HALF],
                                    ALU.add).then_inc(e2_ready, 1)
            v.tensor_tensor(qmean[:, :, :], acc[:, :, :, 0], acc[:, :, :, 1], ALU.add)
            dve.wait_ge(head_sums, 2 * B)
            link(v.tensor_copy(energy[:, 0:NRE[0]], bank[4][0:BH, 0:NRE[0]]))
            link(v.tensor_copy(energy[:, NRE[0]:NF], bank[5][0:BH, 0:NRE[1]]))
            v.tensor_scalar(qmean[:, :, :], qmean[:, :, :], 1.0 / NF, None, ALU.mult).then_inc(qmean_ready, 1)
            for _i in range(KTOP // 8):
                link(v.max(top8[:, :], energy[:, :]))
                link(v.match_replace(energy[:, :], top8[:, :], energy[:, :], -1.0))
            v.tensor_scalar(nsel[:, NF:NF + 1], energy[:, 0:1], 0.0, None, ALU.is_ge)
            v.tensor_scalar(nsel[:, 0:NF], energy[:, :], 0.0, None, ALU.is_ge).then_inc(nsel_ready, 1)
            dve.wait_ge(nsel_ready, 1)
            for s, (lo, hi) in enumerate(((0, NRE[0]), (NRE[0], NF))):
                ins = v.scalar_tensor_tensor(out=masked[:, lo:hi], in0=nsel[:, lo:hi].bitcast(F32), scalar=-NEVER,
                                             in1=bank[6 + s][0:BH, 0:hi - lo], op0=ALU.mult, op1=ALU.add)
            ins.then_inc(en_read, 1)
            dve.wait_ge(en_read, 1)
            link(v.tensor_reduce(hstat[:, 0:1], masked[:, :], AX.X, ALU.max))
            v.tensor_scalar(hstat[:, 1:2], hstat[:, 0:1], -1.0 / (DH ** 0.5 + 1e-8), None,
                            ALU.mult).then_inc(smax_ready, 1)
            dve.wait_ge(exp_ready, 1)
            link(v.reciprocal(hstat[:, 3:4], hstat[:, 2:3]))
            v.tensor_scalar(attn[:, :], attn[:, :], hstat[:, 3:4], None, ALU.mult).then_inc(attn_ready, 1)
            dve.wait_ge(raw_lo, 2)
            for i in range(2 * B):
                par, b = i // B, i % B
                n = NRE[par]
                dve.wait_ge(spread, i + 1)
                link(v.tensor_tensor(av[:, 0:n], bank[b % 2][:, 0:n],
                                     vf[:, b, par * NRE[0]:par * NRE[0] + n], ALU.mult))
                dve.wait_ge(oim_ready, i + 1)
                v.scalar_tensor_tensor(out=of[:, b, par, 0:n], in0=bank[2 + b % 2][:, par:par + n],
                                       scalar=qmean[:, 0, b:b + 1], in1=av[:, 0:n],
                                       op0=ALU.mult, op1=ALU.add).then_inc(ore_ready, 1)
                dve.wait_ge(ore_ready, i + 1)
            dve.wait_ge(y_act, 1)
            v.tensor_tensor(yf[0:1, 0, :], yf[0:1, 0, :], bol[:, :], ALU.add).then_inc(y_fixed, 1)

            def block_out(a):
                dve.wait_ge(inv_even, a + 1)
                ev = bank[a % 2][:, :].rearrange("p (b d) -> p b d", b=B)
                od = bank[2 + a % 2][:, :].rearrange("p (b d) -> p b d", b=B)
                ts = [tsum[:, s, :].rearrange("p (b d) -> p b d", b=B) for s in range(2)]
                v.tensor_tensor(ts[0], x_sb[:, :, a, :], ev, ALU.add)
                link(v.tensor_tensor(ts[1], x_sb[:, :, a + AH, :], ev, ALU.add))
                dve.wait_ge(inv_odd, a + 1)
                v.tensor_tensor(x_sb[:, :, a, :], ts[0], od, ALU.add)
                v.tensor_tensor(x_sb[:, :, a + AH, :], ts[1], od, ALU.subtract).then_inc(inv_read, 1)
                dve.wait_ge(inv_read, a + 1)
                ln_stats(a)
                dve.wait_ge(std_ready, AH + a + 1)
                if a >= 1:
                    dve.wait_ge(xn_ready, AH + a)
                    dve.wait_ge(xn_act, a)
                link(v.reciprocal(lns[:, 5], lns[:, 5]))
                v.scalar_tensor_tensor(out=lns[:, 7], in0=lns[:, 6], scalar=-1.0, in1=lns[:, 5],
                                       op0=ALU.mult, op1=ALU.mult).then_inc(shift_ready, 1)
                for b in range(2, B):
                    for s, t in enumerate((a, a + AH)):
                        ins = v.tensor_scalar(xn[:, t, b, :], x_sb[:, b, t, :], lns[:, 6, b, s:s + 1],
                                              lns[:, 5, b, s:s + 1], ALU.subtract, ALU.mult)
                ins.then_inc(xn_ready, 1)

            def modulate(g):
                dve.wait_ge(tr_mm, g + 1)
                for b in range(2, B):
                    v.tensor_scalar(batch(h2t, g, b),
                                    bank[5][:, 2 * P * (b - 2):2 * P * (b - 1)].rearrange("p (s q) -> p s q", s=2),
                                    camod[:, 1, b:b + 1], mods[:, 3, b:b + 1], ALU.mult, ALU.add).then_inc(h2_dve, 1)

            def largest(g):
                dve.wait_ge(logit_mm, g + 1)
                link(v.tensor_reduce(sm[:, g % 2, 0, :], logit_bank[g][:, :].rearrange("p (j e) -> p j e", e=E),
                                     AX.X, ALU.max))
                v.tensor_scalar(sm[:, g % 2, 1, :], sm[:, g % 2, 0, :], -1.0, None, ALU.mult).then_inc(max_ready, 1)

            def normalise(g):
                dve.wait_ge(rexp, g + 1)
                link(v.reciprocal(sm[:, g % 2, 3, :], sm[:, g % 2, 2, :]))
                for h in range(2):
                    ins = v.tensor_tensor(prob[:, g:HT // P:AH, h, :], logit[:, g % 2, 4 * h:4 * h + 4, :],
                                          sm[:, g % 2, 3, 4 * h:4 * h + 4].unsqueeze(2).broadcast_to([P, 4, E]),
                                          ALU.mult)
                ins.then_inc(prob_ready, 1)

            def make_keys(g):
                dve.wait_ge(probt_ready, g + 1)
                link(v.tensor_scalar(group(keys[:, 0, :], g), group(probt[:, :], g), cst_sb[:, C_SGN:C_SGN + 1], None,
                                     ALU.mult))

            block_out(0)
            block_out(1)
            modulate(0)
            block_out(2)
            largest(0)
            modulate(1)
            block_out(3)
            largest(1)
            modulate(2)
            normalise(0)
            largest(2)
            modulate(3)
            normalise(1)
            largest(3)
            make_keys(0)
            normalise(2)
            make_keys(1)
            normalise(3)
            make_keys(2)
            make_keys(3)
            dve.sem_inc(keys_made, 1)

            def product(q):
                dve.wait_ge(silu_ready, 2 * q + 4)
                dve.wait_ge(gate_kept, 2 * q + 2 + RING)
                dve.wait_ge(put_off[q % RING], 16 * (q // RING + 1))
                v.tensor_tensor(held[:, q % RING], silu[:, q % 2], gate[:, q % 2], ALU.mult).then_inc(pair_made, 1)

            copies, made = 0, 0
            for i, (m, d, pairs) in enumerate(plan):
                if i >= 1:
                    dve.wait_ge(sort_step, i)
                if copies:
                    dve.wait_ge(sort_copy, copies)
                lo = 0 if d == m else d
                src, dst = (keys[:, b, :].rearrange("p (n r) -> p n r", r=2 * m)[:, :, lo:2 * m - lo].rearrange(
                    "p n (g two d) -> p n g two d", two=2, d=d) for b in (i % 2, 1 - i % 2))
                v.tensor_tensor(dst[:, :, :, 0, :], src[:, :, :, 0, :], src[:, :, :, 1, :], ALU.max)
                v.tensor_tensor(dst[:, :, :, 1, :], src[:, :, :, 0, :], src[:, :, :, 1, :],
                                ALU.min).then_inc(sort_step, 1)
                if pairs:
                    product(made)
                    made += pairs
                if d < m:
                    copies += 1
            dve.wait_ge(sort_step, len(plan))
            dve.wait_ge(sort_copy, copies)
            cur = len(plan) % 2

            def exchange(src, dst, d):
                s = keys[:, src, :].rearrange("p (m two d) -> p m two d", two=2, d=d)
                o = keys[:, dst, :].rearrange("p (m two d) -> p m two d", two=2, d=d)
                v.tensor_tensor(o[:, :, 0, :], s[:, :, 0, :], s[:, :, 1, :], ALU.max)
                link(v.tensor_tensor(o[:, :, 1, :], s[:, :, 0, :], s[:, :, 1, :], ALU.min))

            dve.wait_ge(h2_lo, NCH)
            dve.sem_inc(rows_sorted, 1)
            link(v.tensor_copy(swapped[0:E, :], keys[E:P, cur, :]))
            dve.wait_ge(rows_copied, 1)
            link(v.scalar_tensor_tensor(out=keys[:, 1 - cur, :], in0=swapped[:, :], scalar=-1.0,
                                        in1=keys[:, cur, :], op0=ALU.mult, op1=ALU.max))
            cur = 1 - cur
            d = HT // 2
            while d >= G:
                exchange(cur, 1 - cur, d)
                cur = 1 - cur
                d //= 2
            assert cur == (len(plan) + 1 + HALF_STEPS) % 2
            dve.sem_inc(groups_sorted, 1)
            link(v.tensor_reduce(gsum[:, :], keys[:, cur, :].rearrange("p (q g) -> p q g", g=G), AX.X, ALU.add))
            v.tensor_scalar(gsum[:, :], gsum[:, :], cst_sb[:, C_SGN:C_SGN + 1], None, ALU.mult)
            dve.wait_ge(signs_back, 1)
            gv = swapped[:, :].rearrange("p (q g) -> p q g", g=G)
            v.tensor_reduce(gmin[:, :], gv, AX.X, ALU.min)
            link(v.memset(tau[:, :], 0.0))
            for r in range(len(SHIFTS)):
                ti = tau[:, :].bitcast(I32).broadcast_to([P, RATIO])
                link(v.tensor_tensor(cand[:, :].bitcast(I32), ti, bits_sb[:, RATIO * r:RATIO * (r + 1)],
                                     ALU.bitwise_or))
                link(v.tensor_tensor(cmp[:, :, :], gsum[:, :].unsqueeze(1).broadcast_to([P, RATIO, NG]),
                                     cand[:, :].unsqueeze(2).broadcast_to([P, RATIO, NG]), ALU.is_ge))
                v.tensor_reduce(cnt[:, :], cmp[:, :, :], AX.X, ALU.add).then_inc(cmp_done, 1)
                product(made + r)
                dve.wait_ge(cnt_mm, r + 1)
                link(v.scalar_tensor_tensor(out=hit[:, :], in0=bank[7][:, 0:RATIO], scalar=float(GROUPS),
                                            in1=cand[:, :], op0=ALU.is_ge, op1=ALU.mult))
                link(v.tensor_reduce(tau[:, :], hit[:, :], AX.X, ALU.max))
            link(v.tensor_scalar(gpen[:, :], gsum[:, :], tau[:, 0:1], NEVER, ALU.is_lt, ALU.mult))
            link(v.tensor_tensor(gpen[:, :], gpen[:, :], gmin[:, :], ALU.max))
            link(v.tensor_reduce(vth[:, 0:1], gpen[:, :], AX.X, ALU.min))
            v.tensor_copy(vth[0:E, 1:2], vth[E:P, 0:1])
            link(v.tensor_copy(vth[E:P, 1:2], vth[0:E, 0:1]))
            link(v.tensor_tensor(vth[:, 2:3], vth[:, 0:1], vth[:, 1:2], ALU.min))
            xt = x_sb[:, :, :, :].rearrange("p b a d -> p (b a) d")
            dve.wait_ge(scores_dup, 64)

            def keep(c):
                g = gated[:, CH * c:CH * (c + 1)]
                v.scalar_tensor_tensor(out=g, in0=g, scalar=vth[:, 2:3], in1=g,
                                       op0=ALU.is_ge, op1=ALU.mult).then_inc(kept_ready, 1)

            def results(n, s):
                dve.wait_ge(turned, n * 2 + (s + 3))
                dve.wait_ge(stored[s], n * 16 + 16)
                for j in range(TPC):
                    t = bass.ds(n * (2 * TPC) + (s * TPC + j), 1)
                    v.scalar_tensor_tensor(out=res[:, s, j, :], in0=bank[6 + s][:, P * j:P * (j + 1)],
                                           scalar=rden[:, j, bass.ds(n * 2 + s, 1)],
                                           in1=xt[:, t, :].rearrange("p o d -> p (o d)"),
                                           op0=ALU.mult, op1=ALU.add).then_inc(res_ready, 1)

            def hidden(n, first):
                for s in range(2):
                    for k in range(KT):
                        if k % 2 == 0:
                            dve.wait_ge(fetched[k // 2], n * 32 + 16 * (s + 1))
                        dve.wait_ge(down_mm, n * (2 * KT) + (s * KT + k + 1))
                        v.tensor_tensor(hid[:, k % RING], back[:, k // 2, k % 2],
                                        gated[:, bass.ds(n * (2 * CH) + s * CH, CH)],
                                        ALU.mult).then_inc(hid_ready, 1)
                        if first and s == 0 and k < NCH - 1:
                            keep(k + 1)
                        if first and s == 0 and k == 10:
                            dve.wait_ge(den_rows, 1)
                            v.tensor_copy(den_sb[:, :], bank[7][0:NCH, :]).then_inc(den_kept, 1)
                        if first and s == 0 and k == 14:
                            dve.wait_ge(den_turned, 1)
                            link(v.tensor_scalar(rden[:, :, :], bank[7][:, 0:TPC * NCH].rearrange(
                                "p (j n) -> p j n", n=NCH), 1e-6, None, ALU.add))
                            link(v.reciprocal(rden[:, :, :], rden[:, :, :]))
                            dve.wait_ge(kept_ready, NCH)
                        if k == KT // 2 and not (first and s == 0):
                            if s == 0:
                                results(n - 1, 1)
                            else:
                                results(n, 0)

            keep(0)
            dve.wait_ge(kept_ready, 1)
            hidden(0, True)
            with dve.Fori(1, NCH // 2) as n:
                hidden(n, False)
            results(NCH // 2 - 1, 1)

        @block.tensor
        def _(pe):
            mm = nc.tensor.matmul

            pe.wait_ge(ld_mod, 16)
            pe.wait_ge(sc_done, 1)
            for m in range(6):
                mm(bank[6][:, B * m:B * (m + 1)], wmod_sb[:, D * m:D * (m + 1)], sc[:, :], start=True, stop=True)
            pe.wait_ge(scb_done, 1)
            for b in range(B):
                last = mm(bank[7][:, D * b:D * (b + 1)], scb[:, b, :], wmod_sb[:, 2 * D:3 * D],
                          start=True, stop=True)
            last.then_inc(mod_mm, 1)

            for a in range(AH):
                pe.wait_ge(ld_tabf[a], 16)
                pe.wait_ge(plus_ready, a + 1)
                pe.wait_ge(minus_ready, a + 1)
                for b in range(B):
                    if a == 0 and b == B - 1:
                        pe.wait_ge(mod_read, 1)
                    for par in range(2):
                        last = mm(bank[2 * b + par][:, :], fold[:, par, a, D * b:D * (b + 1)],
                                  tabf_sb[:, a, par, :], start=(a == 0), stop=(a == AH - 1))
                        if a == AH - 1:
                            last.then_inc(fwd_ready, 1)

            def project(i):
                b, par = i // 2, i % 2
                n = NRE[par]
                pe.wait_ge(xf_fixed, b + 1)
                pe.wait_ge(xf_dve, b + 1)
                for s, (done, bk, width, w) in enumerate(((q_mm, bank[par], HALF, W_Q), (k_mm, bank[2], n, W_K),
                                                          (v_mm, bank[3], n, W_V))):
                    if i == 0 and s == 1:
                        pe.wait_ge(xf_act, 2)
                    if i == 0 and s == 2:
                        pe.wait_ge(xf_dve, 2)
                    if s == 0 and i >= 2:
                        pe.wait_ge(sq_ready, i - 1)
                    if s == 1 and i >= 1:
                        pe.wait_ge(prod_ready, i)
                    if s == 2 and i >= 1:
                        pe.wait_ge(v_kept, i)
                    last = mm(bk[:, 0:width], wqkv_sb[:, s, :], xf[:, b, par, 0:width],
                              start=True, stop=(par == 1), skip_group_check=True)
                    if par == 0:
                        last = mm(bk[:, 0:1], rows_sb[0:1, w:w + D], rows_sb[0:1, W_L:W_L + 1],
                                  start=False, stop=True, skip_group_check=True)
                    last.then_inc(done, 1)

            def sum_heads(i):
                b, par = i // 2, i % 2
                n = NRE[par]
                sel = sel_sb[:, S_SEL + BH * b:S_SEL + BH * (b + 1)]
                if i == 0:
                    pe.wait_ge(ld_sel, 16)
                    pe.wait_ge(xf_act, B)
                    pe.wait_ge(xf_dve, B)
                pe.wait_ge(mag_ready, i + 1)
                mm(bank[4 + par][0:BH, 0:n], sel, mag[:, par, 0:n], start=(b == 0), stop=(b == B - 1))
                pe.wait_ge(prod_ready, i + 1)
                mm(bank[6 + par][0:BH, 0:n], sel, prodqk[:, par, 0:n], start=(b == 0),
                   stop=(b == B - 1)).then_inc(head_sums, 1)

            pe.wait_ge(ld_w, 32)
            for i in range(2 * B):
                project(i)
                if i >= 2:
                    sum_heads(i - 2)
            sum_heads(2 * B - 2)
            sum_heads(2 * B - 1)

            pe.wait_ge(nsel_ready, 1)
            pe.wait_ge(sel_ready, 1)
            pe.wait_ge(attn_ready, 1)

            def spread_heads(i):
                par, b = i // B, i % B
                n, lo = NRE[par], par * NRE[0]
                if i >= 2:
                    pe.wait_ge(ore_ready, i - 1)
                    pe.wait_ge(oim_ready, i - 1)
                exp = sel_sb[0:BH, S_EXP + P * b:S_EXP + P * (b + 1)]
                mm(bank[b % 2][:, 0:n], exp, attn[:, lo:lo + n], start=True, stop=True)
                mm(bank[2 + b % 2][:, 0:NRE[0] + 1], exp_sel[:, P * b:P * (b + 1)],
                   nsel[:, lo - par:lo - par + NRE[0] + 1], start=True, stop=True).then_inc(spread, 1)

            def project_out(i):
                par = i // AH
                pe.wait_ge(ore_ready, B * (par + 1))
                pe.wait_ge(oim_ready, B * (par + 1))
                if i >= 4:
                    pe.wait_ge(y_act, i - 3)
                for b in range(B):
                    last = mm(bank[4 + i % 4][:, D * b:D * (b + 1)], of[:, b, par, P * (i % AH):P * (i % AH + 1)],
                              wob[:, b, :], start=True, stop=True)
                last.then_inc(y_mm, 1)

            for i in range(B + 1):
                spread_heads(i)
            for i in range(1, B):
                spread_heads(B + i)
                project_out(i - 1)
            for i in range(B - 1, A):
                project_out(i)

            pe.wait_ge(ld_tabi, 16)
            pe.wait_ge(y_fixed, 1)

            def inverse(a):
                if a >= 2:
                    pe.wait_ge(inv_read, a - 1)
                for par, done in enumerate((inv_even, inv_odd)):
                    for i in range(AH * par, AH * (par + 1)):
                        pe.wait_ge(y_act, i + 1)
                        last = mm(bank[2 * par + a % 2][:, :], tabi_sb[:, i, P * a:P * (a + 1)], yf[:, i, :],
                                  start=(i == AH * par), stop=(i == AH * (par + 1) - 1))
                    last.then_inc(done, 1)

            def turn_in(g):
                pe.wait_ge(xn_ready, AH + g + 1)
                pe.wait_ge(xn_act, g + 1)
                if g >= 1:
                    pe.wait_ge(h2_act, 2 * g)
                    pe.wait_ge(h2_dve, 2 * g)
                for b in range(B):
                    for s in range(2):
                        c = P * (2 * (b % 2) + s)
                        last = nc.tensor.transpose(bank[4 + b // 2][:, c:c + P], xn[:, g + AH * s, b, :], ident)
                last.then_inc(tr_mm, 1)

            def logits(g):
                if g in (1, 2):
                    pe.wait_ge(inv_read, AH - 1)
                if g == 3:
                    pe.wait_ge(rexp, 1)
                mm(logit_bank[g][:, :], ones[0:1, :], br_sb[:, :].unsqueeze(1).broadcast_to([1, 8, E]),
                   start=True, stop=False, skip_group_check=True)
                pe.wait_ge(h2_act, 2 * (g + 1))
                pe.wait_ge(h2_dve, 2 * (g + 1))
                for j in range(NCH):
                    c = CH * j + P * g
                    last = mm(logit_bank[g][:, E * j:E * (j + 1)], h2t[:, c:c + P], wr_sb[:, :], start=False,
                              stop=(j == 7), skip_group_check=True)
                last.then_inc(logit_mm, 1)

            def turn_probs(g):
                pe.wait_ge(prob_ready, g + 1)
                if g >= 1:
                    pe.wait_ge(probt_ready, g)
                for q in range(4):
                    last = nc.tensor.transpose(bank[7][:, P * q:P * (q + 1)],
                                               prob[:, AH * q + g, :, :].rearrange("p h e -> p (h e)"), ident)
                last.then_inc(prob_tr, 1)

            inverse(0)
            inverse(1)
            pe.wait_ge(ld_cst, 16)
            pe.wait_ge(ld_ffn, 48)
            turn_in(0)
            inverse(2)
            logits(0)
            turn_in(1)
            inverse(3)
            logits(1)
            turn_in(2)
            logits(2)
            turn_in(3)
            turn_probs(0)
            logits(3)
            turn_probs(1)
            turn_probs(2)
            turn_probs(3)

            def product3(out_, w_hi, w_lo, m_hi, m_lo, alone=True):
                mm(out_, w_hi, m_hi, start=alone, stop=False)
                mm(out_, w_lo, m_hi, start=False, stop=False)
                return mm(out_, w_hi, m_lo, start=False, stop=alone)

            pe.wait_ge(raw_lo, 2)

            def up_gate(n, k):
                hi, lo = h2hi[:, bass.ds(n * CH, CH)], h2lo[:, bass.ds(n * CH, CH)]
                pe.wait_ge(silu_ready, n * KT + (k + 1))
                product3(bank[k % 2][:, :], wup_hi[:, k], wup_lo[:, k], hi, lo).then_inc(up_mm, 1)
                pe.wait_ge(gate_kept, n * KT + (k + 1))
                product3(bank[2 + k % RING][:, :], wgate_hi[:, k], wgate_lo[:, k], hi, lo).then_inc(gate_mm, 1)

            with pe.Fori(0, NCH - 1) as n:
                pe.wait_ge(h2_lo, n + 1)
                for k in range(KT):
                    up_gate(n, k)
            pe.wait_ge(probt_ready, 4)
            pe.wait_ge(h2_lo, NCH)
            for k in range(RING):
                up_gate(NCH - 1, k)
            for r in range(len(SHIFTS)):
                pe.wait_ge(cmp_done, r + 1)
                mm(bank[7][:, 0:RATIO], ones, cnt[:, :], start=True, stop=True).then_inc(cnt_mm, 1)
                for k in (2 * r + RING, 2 * r + RING + 1):
                    if k < KT:
                        up_gate(NCH - 1, k)
            pe.wait_ge(silu_ready, NCH * KT + 2)
            pe.wait_ge(gate_kept, NCH * KT + RING)

            def turn_back(n, s):
                pe.wait_ge(out_ready, n * 2 + (s + 1))
                pe.wait_ge(res_ready, n * (2 * TPC) + (s + 1) * TPC)
                for j in range(TPC):
                    last = nc.tensor.transpose(bank[6 + s][:, P * j:P * (j + 1)],
                                               outt[:, s, P * j:P * (j + 1)], ident)
                last.then_inc(turned, 1)

            def serve(n, first):
                for s in range(2):
                    if not first:
                        pe.wait_ge(out_ready, n * 2 + (s - 1))
                    for k in range(KT):
                        pe.wait_ge(hid_ready, n * (2 * KT) + (s * KT + k + 1 + 2 * BACK))
                        mm(bank[4 + s][:, :], wdown_sb[:, k], hid[:, k % RING], start=(k == 0),
                           stop=(k == KT - 1)).then_inc(down_mm, 1)
                        if k == 4 and not (first and s == 0):
                            if s == 0:
                                turn_back(n - 1, 1)
                            else:
                                turn_back(n, 0)
                        if first and s == 0 and k == 8:
                            pe.wait_ge(kept_lo_ready, NCH)
                            for c in range(NCH):
                                for part in (kept_hi, kept_lo):
                                    last = mm(bank[7][0:NCH, :], row_sel[:, NCH * c:NCH * (c + 1)],
                                              part[:, CH * c:CH * (c + 1)], start=(c == 0 and part is kept_hi),
                                              stop=(c == NCH - 1 and part is kept_lo))
                            last.then_inc(den_rows, 1)
                        if k == 8:
                            c = bass.ds(n * (2 * CH) + s * CH, CH)
                            product3(bank[4 + s][:, :], bdown_hi[:, :], bdown_lo[:, :], kept_hi[:, c],
                                     kept_lo[:, c], alone=False)
                        if first and s == 0 and k == 12:
                            pe.wait_ge(den_kept, 1)
                            for j in range(TPC):
                                last = nc.tensor.transpose(bank[7][:, NCH * j:NCH * (j + 1)],
                                                           den_sb[:, P * j:P * (j + 1)], ident[0:NCH, 0:NCH])
                            last.then_inc(den_turned, 1)

            pe.sem_inc(turned, 2)
            pe.sem_inc(down_mm, RING)
            pe.wait_ge(ld_down, 16)
            pe.wait_ge(raw_lo, 3)
            serve(0, True)
            with pe.Fori(1, NCH // 2) as n:
                serve(n, False)
            turn_back(NCH // 2 - 1, 1)


def kernel(L0_attn_query, L0_attn_Wq, L0_attn_bq, L0_attn_Wk, L0_attn_bk, L0_attn_Wv, L0_attn_bv, L0_attn_Wo,
           L0_attn_bo, L0_ffn_Wr, L0_ffn_br, L0_ffn_Wup, L0_ffn_bup, L0_ffn_Wgate, L0_ffn_bgate, L0_ffn_Wdown,
           L0_ffn_bdown, L0_c, L0_wmod):
    import concourse.bacc as bacc
    from concourse.bass_utils import run_bass_kernel_spmd

    def arr(v):
        return np.ascontiguousarray(np.asarray(v))

    def unit_tiles(v):
        return arr(v).T.reshape(KT, P).T

    tabf, tabi = transform_tables()
    arrays = {
        "x": arr(L0_attn_query),
        "cst": constants(),
        "sel": selectors(),
        "bits": round_bits(),
        "cols": arr(np.concatenate([arr(L0_c).T, unit_tiles(L0_ffn_bup), unit_tiles(L0_ffn_bgate)], axis=1)),
        "rows": arr(np.concatenate([arr(L0_attn_bq), arr(L0_attn_bk), arr(L0_attn_bv), arr(L0_attn_bo),
                                    np.full(1, L, np.float32)])[None, :]),
        "wmod": arr(L0_wmod),
        "wqkv": arr(np.concatenate([arr(L0_attn_Wq), arr(L0_attn_Wk), arr(L0_attn_Wv)], axis=1)),
        "wo": arr(L0_attn_Wo),
        "tabf": tabf,
        "tabi": tabi,
        "wr": arr(L0_ffn_Wr),
        "br": arr(L0_ffn_br),
        "wup": arr(arr(L0_ffn_Wup).transpose(1, 2, 0).reshape(D, E * H)),
        "wgate": arr(arr(L0_ffn_Wgate).transpose(1, 2, 0).reshape(D, E * H)),
        "wdown": arr(arr(L0_ffn_Wdown).transpose(1, 0, 2).reshape(KT, P, D).transpose(1, 0, 2).reshape(P, KT * D)),
        "bdown": arr(L0_ffn_bdown),
    }
    nc = bacc.Bacc("TRN2", target_bir_lowering=False, num_devices=1)
    args = [nc.dram_tensor(f"in_{k}", a.shape, mybir.dt.from_np(a.dtype), kind="ExternalInput").ap()
            for k, a in arrays.items()]
    out = nc.dram_tensor("out_y", (B, L, D), F32, kind="ExternalOutput").ap()
    build(nc, *args, out)
    r = run_bass_kernel_spmd(nc, [{f"in_{k}": a for k, a in arrays.items()}], core_ids=[0])
    return r.results[0]["out_y"]
```
